# Optimizing a Trainium2 kernel written in Bass

```python
import numpy as np
import jax
import jax.numpy as jnp

def _softmax(x, axis=-1):
    return jax.nn.softmax(x, axis=axis)

def _gelu(x):
    return jax.nn.gelu(x, approximate=True)

def _silu(x):
    return jax.nn.silu(x)

def _sigmoid(x):
    return jax.nn.sigmoid(x)

def _layernorm(x, axis=-1, eps=1e-05):
    m = jnp.mean(x, axis=axis, keepdims=True)
    v = jnp.var(x, axis=axis, keepdims=True)
    return (x - m) / jnp.sqrt(v + eps)

def _scatter_add(tgt, idx, src, axis=0):
    return tgt.at[idx].add(src)

def _segment_sum(src, seg, n):
    return jax.ops.segment_sum(src, seg, n)
kernel_name = 'mk_prb_d1_jaxref_r4_83c40a'

def setup_inputs(seed: int=0):
    np.random.seed(seed)
    _w = jnp.asarray

    def _L0_attn_setup():
        import jax, jax.numpy as jnp
        import numpy as np
        import math
        D_MODEL = 512
        N_HEADS = 16
        D_HEAD = D_MODEL // N_HEADS
        MAX_T = 512
        B, T = (2, 512)

        def rotate_half(x):
            x1 = x[..., ::2]
            x2 = x[..., 1::2]
            return jnp.stack((-x2, x1), axis=-1).reshape(x.shape)
        key = jax.random.key(seed)
        k1, k2, k3 = jax.random.split(key, 3)
        x = jax.random.normal(k1, (B, T, D_MODEL), dtype=jnp.float32)
        s = 1.0 / math.sqrt(D_MODEL)
        Wqkv = jax.random.uniform(k2, (3 * D_MODEL, D_MODEL), dtype=jnp.float32, minval=-s, maxval=s)
        WO = jax.random.uniform(k3, (D_MODEL, D_MODEL), dtype=jnp.float32, minval=-s, maxval=s)
        return {'x': x, 'Wqkv': Wqkv, 'WO': WO}
    _L0_attn_in = _L0_attn_setup()

    def _L0_ffn_setup():
        import jax, jax.numpy as jnp
        import numpy as np
        HIDDEN = 512
        INTER = 1408
        B, S = (2, 512)

        def _ternary(key, shape):
            return jax.random.randint(key, shape, -1, 2).astype(jnp.float32)
        key = jax.random.key(seed)
        ks = jax.random.split(key, 7)
        x = jax.random.normal(ks[0], (B, S, HIDDEN), dtype=jnp.float32)
        gate_w = _ternary(ks[1], (INTER, HIDDEN))
        up_w = _ternary(ks[2], (INTER, HIDDEN))
        down_w = _ternary(ks[3], (HIDDEN, INTER))
        gate_s = jax.random.uniform(ks[4], (INTER,), minval=0.01, maxval=0.1, dtype=jnp.float32)
        up_s = jax.random.uniform(ks[5], (INTER,), minval=0.01, maxval=0.1, dtype=jnp.float32)
        down_s = jax.random.uniform(ks[6], (HIDDEN,), minval=0.01, maxval=0.1, dtype=jnp.float32)
        return {'x': x, 'gate_w': gate_w, 'up_w': up_w, 'down_w': down_w, 'gate_s': gate_s, 'up_s': up_s, 'down_s': down_s}
    _L0_ffn_in = _L0_ffn_setup()
    _d = {'L0_attn_x': _L0_attn_in['x'], 'L0_attn_Wqkv': _L0_attn_in['Wqkv'], 'L0_attn_WO': _L0_attn_in['WO'], 'L0_ffn_gate_w': _L0_ffn_in['gate_w'], 'L0_ffn_up_w': _L0_ffn_in['up_w'], 'L0_ffn_down_w': _L0_ffn_in['down_w'], 'L0_ffn_gate_s': _L0_ffn_in['gate_s'], 'L0_ffn_up_s': _L0_ffn_in['up_s'], 'L0_ffn_down_s': _L0_ffn_in['down_s']}
    _x0 = _d['L0_attn_x']
    _d['L0_attn_x'] = jax.random.normal(jax.random.fold_in(jax.random.key(seed), 1), (8, 512, 512), dtype=_x0.dtype)
    del _x0
    return _d

def reference(L0_attn_x, L0_attn_Wqkv, L0_attn_WO, L0_ffn_gate_w, L0_ffn_up_w, L0_ffn_down_w, L0_ffn_gate_s, L0_ffn_up_s, L0_ffn_down_s):

    def _L0_attn_ref(x, Wqkv, WO):
        import jax, jax.numpy as jnp
        import numpy as np
        import math
        D_MODEL = 512
        N_HEADS = 16
        D_HEAD = D_MODEL // N_HEADS
        MAX_T = 512
        B, T = (2, 512)

        def rotate_half(x):
            x1 = x[..., ::2]
            x2 = x[..., 1::2]
            return jnp.stack((-x2, x1), axis=-1).reshape(x.shape)
        Bx, Tx, _ = x.shape
        pos = jnp.arange(Tx, dtype=jnp.float32)
        freqs = jnp.exp(-math.log(10000.0) * jnp.arange(0, D_HEAD, 2, dtype=jnp.float32) / D_HEAD)
        angles = pos[:, None] * freqs[None, :]
        sin = jnp.repeat(jnp.sin(angles), 2, axis=-1)
        cos = jnp.repeat(jnp.cos(angles), 2, axis=-1)
        sin = sin[None, None, :, :]
        cos = cos[None, None, :, :]
        qkv = x @ Wqkv.T
        q, k, v = jnp.split(qkv, 3, axis=-1)

        def to_heads(t):
            return t.reshape(Bx, Tx, N_HEADS, D_HEAD).transpose(0, 2, 1, 3)
        q, k, v = (to_heads(q), to_heads(k), to_heads(v))
        q = q * cos + rotate_half(q) * sin
        k = k * cos + rotate_half(k) * sin
        scores = jnp.einsum('bhqd,bhkd->bhqk', q, k) / math.sqrt(D_HEAD)
        mask = jnp.triu(jnp.full((Tx, Tx), -jnp.inf, dtype=scores.dtype), k=1)
        scores = scores + mask
        attn = jax.nn.softmax(scores, axis=-1)
        out = jnp.einsum('bhqk,bhkd->bhqd', attn, v)
        out = out.transpose(0, 2, 1, 3).reshape(Bx, Tx, D_MODEL)
        return out @ WO.T

    def _L0_ffn_ref(x, gate_w, up_w, down_w, gate_s, up_s, down_s):
        import jax, jax.numpy as jnp
        import numpy as np
        HIDDEN = 512
        INTER = 1408
        B, S = (2, 512)

        def _ternary(key, shape):
            return jax.random.randint(key, shape, -1, 2).astype(jnp.float32)
        b, s, h = x.shape
        xf = x.reshape(b * s, h)
        g = jnp.einsum('th,ih->ti', xf, gate_w) * gate_s
        u = jnp.einsum('th,ih->ti', xf, up_w) * up_s
        hdn = jax.nn.silu(g) * u
        out = jnp.einsum('ti,hi->th', hdn, down_w) * down_s
        return out.reshape(b, s, -1)
    x = L0_attn_x
    xn = _layernorm(x, axis=-1)
    x = x + _L0_attn_ref(xn, L0_attn_Wqkv, L0_attn_WO) + _L0_ffn_ref(xn, L0_ffn_gate_w, L0_ffn_up_w, L0_ffn_down_w, L0_ffn_gate_s, L0_ffn_up_s, L0_ffn_down_s)
    return x

_drawn_inputs = setup_inputs


def setup_inputs(seed=0):
    import zlib

    import numpy as np

    out = dict(_drawn_inputs(seed))
    spreads = {}
    factors = {}
    for name, (base, spread) in spreads.items():
        noise = np.random.default_rng([zlib.crc32(name.encode()), seed]).standard_normal(out[name].shape)
        drawn = base * np.exp(spread * noise) if base else spread * noise
        out[name] = jnp.asarray(drawn.astype(out[name].dtype))
    for name, factor in factors.items():
        out[name] = (out[name] * factor).astype(out[name].dtype)
    return out
```

```python
from contextlib import ExitStack

import numpy as np

import concourse.bass as bass
from concourse import mybir

F32 = mybir.dt.float32
F16 = mybir.dt.float16
BF16 = mybir.dt.bfloat16
ALU = mybir.AluOpType
ACT = mybir.ActivationFunctionType

P = 128
BATCH, SEQ, DIM = 8, 512, 512
HEADS, HD = 16, 32
INNER = 1408
TILES = SEQ // P
KT = DIM // P
GROUPS = HEADS * HD // P
GH = P // HD
CHUNKS = INNER // P
ROWS = GROUPS * TILES
UNITS = ROWS * GH
EPS = 1e-5
HI, LO = 0, 1
TERMS = ((HI, HI), (LO, HI), (HI, LO))

X_SCALE = 2.0 ** 8
W_SCALE = 2.0 ** 10
F_SCALE = 2.0 ** 6
QKV_SCALE = 2.0 ** 6
P_SCALE = 2.0 ** 10
A_SCALE = 2.0 ** 8
H_SCALE = 2.0 ** 4
QKV_OUT = QKV_SCALE / (X_SCALE * W_SCALE)
SCORE = HD ** -0.5 / QKV_SCALE ** 2
A_OUT = A_SCALE / (P_SCALE * QKV_SCALE)
WO_OUT = 1.0 / (A_SCALE * W_SCALE)
G_OUT = 1.0 / (X_SCALE * F_SCALE)
D_OUT = 1.0 / (H_SCALE * F_SCALE)
MASKED = -1e30
START = 1


def main_steps():
    halves = [(k, c) for c in range(CHUNKS) for k in ("gate", "up")]
    a_rows = (GROUPS - 1) * TILES
    steps = [("score", 0)]
    due = 0.0
    for n in range(UNITS):
        row, at = divmod(n, GH)
        if n + 1 < UNITS:
            steps.append(("score", n + 1))
        if row < a_rows:
            at_a = (1 + row // TILES, row % TILES)
            if at == 0:
                steps.append(("project", *at_a))
            if at == 1:
                steps.append(("split_qk", *at_a))
            if at == 2:
                steps.append(("turn_qk", *at_a))
            due += 0.25
        else:
            due += (2 * CHUNKS - a_rows) / (UNITS - a_rows * GH)
        if due >= 1 - 1e-9 and halves:
            due -= 1
            kind, c = halves.pop(0)
            steps.append((kind, c))
            if kind == "up":
                split_after = n + 1
                steps.append(("late", c))
        steps.append(("turn_p", n))
        if n % (GH * TILES) == GH * TILES - 1:
            steps.append(("sums", n // (GH * TILES)))
        if n % GH == 0 and n:
            steps.append(("values", row - 1))
            if row % TILES == 0:
                steps.append(("norm", row // TILES - 1))
    assert not halves
    out, held = [], []
    for s in steps:
        if s[0] == "late":
            held.append(s[1])
            continue
        out.append(s)
        if s[0] == "turn_p":
            out += [("split_h", c) for c in held]
            held = []
    return out + [("values", ROWS - 1), ("norm", GROUPS - 1)]


def tail_steps(more):
    a = [("ln", 0), ("ln", 1), ("down", 0), ("turn_x", 0), ("turn_x", 1), ("ln", 2), ("ln", 3), ("down", 1),
         ("turn_x", 2), ("turn_x", 3), ("down", 2), ("project", 0, 0), ("down", 3), ("split_qk", 0, 0),
         ("project", 0, 1), ("turn_qk", 0, 0), ("out", 0), ("split_qk", 0, 1), ("project", 0, 2),
         ("turn_qk", 0, 1), ("out", 1), ("split_qk", 0, 2), ("project", 0, 3), ("turn_qk", 0, 2), ("out", 2),
         ("split_qk", 0, 3), ("out", 3), ("turn_qk", 0, 3)]
    return a if more else [s for s in a if s[0] in ("down", "out")]


def head_steps():
    out = [("ln", 0), ("ln", 1), ("turn_x", 0), ("ln", 2), ("turn_x", 1), ("ln", 3), ("turn_x", 2), ("turn_x", 3)]
    for t in range(TILES):
        out += [("project", 0, t), ("split_qk", 0, t), ("turn_qk", 0, t)]
    return out


def unit(n):
    return n // (TILES * GH), n // GH % TILES, n % GH


def layer(nc, x, wqkv, wo, wg, wu, wd, gate_s, up_s, down_s, rope, y_out):
    ctx = ExitStack()
    with ctx:
        def sb(name, shape, dtype):
            return ctx.enter_context(nc.sbuf_tensor(name, shape, dtype))

        def pb(name, shape, dtype):
            return ctx.enter_context(nc.psum_tensor(name, shape, dtype))

        def sem(name):
            return ctx.enter_context(nc.semaphore(name))

        wqkv_s = sb("wqkv_s", [P, 2, KT, GROUPS * 3 * P], F16)
        wo_s = sb("wo_s", [P, 2, GROUPS, DIM], F16)
        wg_s = sb("wg_s", [P, 2, KT, INNER], F16)
        wu_s = sb("wu_s", [P, 2, KT, INNER], F16)
        wd_s = sb("wd_s", [P, 2, CHUNKS, DIM], F16)
        ident = sb("ident", [P, P], F32)
        ident16 = sb("ident16", [P, P], F16)
        mask = sb("mask", [P, SEQ], BF16)
        rope_s = sb("rope_s", [P, TILES, 2, HD], F32)
        down_row = sb("down_row", [P, DIM], F32)
        gate_half = sb("gate_half", [P, CHUNKS], F32)
        gate_up = sb("gate_up", [P, CHUNKS], F32)
        neg_half = sb("neg_half", [P, 1], F32)
        x_in = sb("x_in", [P, 2, DIM], F32)
        stats = sb("stats", [P, 2, 6], F32)
        mean_var = sb("mean_var", [P, 2, 2], F32)
        rstd = sb("rstd", [P, 2, 2], F32)
        xT = sb("xT", [P, 2, KT, SEQ], F16)
        x_cos = sb("x_cos", [P, 2 * P], F32)
        x_sin = sb("x_sin", [P, 2 * P], F32)
        qk = sb("qk", [P, 2, 2 * P], F32)
        qk_parts = sb("qk_parts", [P, 2, 2, GH, 4, HD], F16)
        qkT = sb("qkT", [P, 2, TILES, 2, GH, P], F16)
        v = sb("v", [P, 2, 2, TILES, P], F16)
        neg_max = sb("neg_max", [P, 4], F32)
        probs = sb("probs", [P, 2, SEQ], F32)
        pT = sb("pT", [P, 2, GH, 2, SEQ], F16)
        sums = sb("sums", [P, 2, TILES * GH], F32)
        inv = sb("inv", [P, TILES * GH], F32)
        spread = sb("spread", [P, SEQ], F32)
        aT = sb("aT", [P, 2, GROUPS, SEQ], F16)
        tanh = sb("tanh", [P, SEQ], F32)
        inner = sb("inner", [P, 2, SEQ], F32)
        hT = sb("hT", [P, 2, CHUNKS, SEQ], F16)
        x_res = sb("x_res", [P, 2, DIM], F32)
        y = pT[:, 0, :, :, :].rearrange("p h s q -> p (h s q)").bitcast(F32).rearrange("p (t d) -> p t d", t=TILES)
        staging = hT[:, :, :, :].rearrange("p s c q -> p (s c q)").bitcast(F32).rearrange("p (r w) -> p r w", r=2)

        ps_s = [pb("ps_s0", [P, 512], F32), pb("ps_s1", [P, 512], F32)]
        ps_t = pb("ps_t", [P, 512], F32)
        ps_o = pb("ps_o", [P, 512], F32)
        ps_a = pb("ps_a", [P, 512], F32)
        ps_q = pb("ps_q", [P, 1024], F16)
        ps_f = [pb("ps_f0", [P, 512], F32), pb("ps_f1", [P, 512], F32)]

        consts_loaded = sem("consts_loaded")
        consts_done = sem("consts_done")
        scales_done = sem("scales_done")
        w_loaded = [sem("w_loaded0"), sem("w_loaded1")]
        w_hi = sem("w_hi")
        w_lo = sem("w_lo")
        x_loaded = [sem("x_loaded0"), sem("x_loaded1")]
        res_loaded = [sem("res_loaded0"), sem("res_loaded1")]
        stored = sem("stored")
        scored = sem("scored")
        p_turned = sem("p_turned")
        valued = sem("valued")
        inv_turned = sem("inv_turned")
        projected = sem("projected")
        qk_turned = sem("qk_turned")
        gated = sem("gated")
        upped = sem("upped")
        x_turned = sem("x_turned")
        downed = sem("downed")
        outed = sem("outed")
        stats_done = sem("stats_done")
        var_done = sem("var_done")
        x_normed = sem("x_normed")
        xT_lo = sem("xT_lo")
        rotated = sem("rotated")
        v_lo = sem("v_lo")
        qkT_done = sem("qkT_done")
        max_done = sem("max_done")
        pT_lo = sem("pT_lo")
        inv_done = sem("inv_done")
        attended = sem("attended")
        inner_g = sem("inner_g")
        inner_gu = sem("inner_gu")
        y_down = sem("y_down")
        y_done = sem("y_done")
        xT_hi = sem("xT_hi")
        v_hi = sem("v_hi")
        qk_hi = sem("qk_hi")
        exp_done = sem("exp_done")
        pT_hi = sem("pT_hi")
        inv_back = sem("inv_back")
        aT_hi = sem("aT_hi")
        tanh_done = sem("tanh_done")
        hT_hi = sem("hT_hi")
        rstd_done = sem("rstd_done")
        qk_summed = sem("qk_summed")
        qk_lo = sem("qk_lo")
        inv_spread = sem("inv_spread")
        aT_lo = sem("aT_lo")
        hT_lo = sem("hT_lo")
        y_x = sem("y_x")

        dve_passed = sem("dve_passed")
        pool_passed = sem("pool_passed")

        def flat(w, part):
            return w[:, part, :, :].rearrange("p a n -> p (a n)")

        pieces = []
        for src, dst, scale, cut in ((wqkv, wqkv_s, W_SCALE, 3), (wo, wo_s, W_SCALE, 1), (wg, wg_s, F_SCALE, 2),
                                     (wu, wu_s, F_SCALE, 2), (wd, wd_s, F_SCALE, 2)):
            width = src.shape[1] // cut
            pieces += [(src, dst, scale, k * width, width) for k in range(cut)]

        x_v = x.rearrange("b (t p) d -> b p t d", p=P)
        y_v = y_out.rearrange("b (t p) d -> b p t d", p=P)

        block = ctx.enter_context(nc.Block())

        @block.sync
        def _(sp):
            def load_x(b, t, wait=True):
                if wait:
                    sp.wait_ge(x_turned, START + b * TILES + t - 1)
                sp.dma_start(x_in[:, t % 2, :], x_v[b][:, t, :]).then_inc(x_loaded[t % 2], 16)

            def load_res(b, t):
                sp.wait_ge(y_x, START + b * TILES + (t - 1 if t >= 2 else 0))
                sp.dma_start(x_res[:, t % 2, :], x_v[b][:, t, :]).then_inc(res_loaded[t % 2], 16)

            def steps(b, todo):
                for s in todo:
                    if s == ("turn_x", 0) or s == ("turn_x", 1):
                        load_x(b + 1, s[1] + 2)
                    elif s == ("down", 0) or s == ("down", 1):
                        load_res(b, s[1] + 2)
                    elif s[0] == "out":
                        t = s[1]
                        sp.wait_ge(y_done, START + b * TILES + t + 1)
                        sp.dma_start(y_v[b][:, t, :], y[:, t, :]).then_inc(stored, 16)

            sp.sem_inc(stored, START)
            load_x(0, 0, wait=False)
            load_x(0, 1, wait=False)
            sp.dma_start(rope_s[:, :, :, :], rope).then_inc(consts_loaded, 16)
            sp.dma_start(gate_half[:, :], gate_s).then_inc(consts_loaded, 16)
            sp.dma_start(gate_up[:, :], up_s).then_inc(consts_loaded, 16)
            sp.dma_start(down_row[:, :], down_s.broadcast_to([P, DIM])).then_inc(consts_loaded, 16)
            for k, (src, dst, scale, at, width) in enumerate(pieces):
                if k >= 2:
                    sp.wait_ge(w_lo, k - 1)
                sp.dma_start(staging[:, k % 2, 0:width], src[:, at:at + width]).then_inc(w_loaded[k % 2], 16)
            load_x(0, 2)
            load_x(0, 3)
            with sp.Fori(0, BATCH - 1) as b:
                load_res(b, 0)
                load_res(b, 1)
                load_x(b + 1, 0)
                load_x(b + 1, 1)
                steps(b, tail_steps(True))
            load_res(BATCH - 1, 0)
            load_res(BATCH - 1, 1)
            steps(BATCH - 1, tail_steps(False))
            sp.wait_ge(stored, START + 16 * BATCH * TILES)

        @block.tensor
        def _(pe):
            def product(ps, pairs, sem_done):
                for k, (stationary, moving) in enumerate(pairs):
                    last = nc.tensor.matmul(ps, stationary, moving, start=(k == 0), stop=(k == len(pairs) - 1))
                last.then_inc(sem_done, 1)

            def turn_x(b, t, first=False):
                pe.wait_ge(x_normed, START + b * TILES + t + 1)
                if t >= 2:
                    pe.wait_ge(xT_lo, START + b * TILES + t - 1)
                elif not first:
                    pe.wait_ge(exp_done, START + (b - 1) * UNITS + UNITS - 1 + t)
                for k in range(KT):
                    last = nc.tensor.transpose(ps_s[t % 2][:, k * P:(k + 1) * P], x_in[:, t % 2, k * P:(k + 1) * P],
                                               ident[:, :])
                last.then_inc(x_turned, 1)

            def project(b, g, t, first=False):
                a = b * ROWS + g * TILES + t
                pe.wait_ge(xT_lo, START + b * TILES + t + 1)
                if not (first and t == 0):
                    pe.wait_ge(v_lo, START + a)
                product(ps_a[:, 0:3 * P],
                        [(xT[:, xp, k, t * P:(t + 1) * P], wqkv_s[:, wp, k, g * 3 * P:(g + 1) * 3 * P])
                         for k in range(KT) for xp, wp in TERMS], projected)

            def turn_qk(b, g, t):
                a = b * ROWS + g * TILES + t
                pe.wait_ge(qk_lo, START + 2 * a + 2)
                pe.wait_ge(qkT_done, START + a)
                for q in range(2):
                    for h in range(GH):
                        last = nc.tensor.transpose(
                            ps_q[:, (q * GH + h) * P:(q * GH + h + 1) * P],
                            qk_parts[:, t % 2, q, h, :, :].rearrange("p s d -> p (s d)"), ident16[:, :])
                last.then_inc(qk_turned, 1)

            def score(b, n):
                g, i, h = unit(n)
                pe.wait_ge(qkT_done, START + b * ROWS + n // GH + 1)
                if n < 2:
                    pe.wait_ge(xT_lo, START + b * TILES + TILES)
                else:
                    pe.wait_ge(exp_done, START + b * UNITS + n - 1)
                nc.tensor.matmul(ps_s[n % 2][:, 0:(i + 1) * P], qkT[:, g % 2, i, 0, h, :],
                                 qkT[:, g % 2, 0:i + 1, 1, h, :], start=True, stop=True).then_inc(scored, 1)

            def turn_p(b, n):
                g, i, h = unit(n)
                pe.wait_ge(exp_done, START + b * UNITS + n + 1)
                pe.wait_ge(pT_lo, START + b * UNITS + n)
                if n == 0:
                    pe.wait_ge(y_done, START + b * TILES)
                if n % (TILES * GH) == 1 and n > 1:
                    pe.wait_ge(inv_back, START + b * GROUPS + g)
                for j in range(i + 1):
                    last = nc.tensor.transpose(ps_t[:, j * P:(j + 1) * P], probs[:, n % 2, j * P:(j + 1) * P],
                                               ident[:, :])
                last.then_inc(p_turned, 1)

            def values(b, row):
                g, i = divmod(row, TILES)
                pe.wait_ge(pT_lo, START + b * UNITS + (row + 1) * GH)
                pe.wait_ge(v_lo, START + b * ROWS + row + 1)
                if i == 0:
                    pe.wait_ge(attended, START + b * GROUPS + g)
                    pe.wait_ge(y_done, START + b * TILES)
                for j in range(i + 1):
                    for k, (pp, vp) in enumerate(TERMS):
                        for h in range(GH):
                            last = nc.tensor.matmul(
                                ps_o[h * HD:(h + 1) * HD, i * P:(i + 1) * P], v[:, g % 2, vp, j, h * HD:(h + 1) * HD],
                                pT[:, row % 2, h, pp, j * P:(j + 1) * P],
                                start=(j == 0 and k == 0), stop=(j == i and k == len(TERMS) - 1))
                last.then_inc(valued, 1)

            def norm(b, g):
                pe.wait_ge(inv_spread, START + b * GROUPS + g + 1)
                pe.wait_ge(pT_lo, START + b * UNITS + min((g + 1) * TILES * GH + 1, UNITS))
                for i in range(TILES):
                    last = nc.tensor.transpose(ps_t[:, i * P:(i + 1) * P], spread[:, i * P:(i + 1) * P], ident[:, :])
                last.then_inc(inv_turned, 1)

            def inner_half(b, c, w, ps, bank_read, sem_done):
                pe.wait_ge(xT_lo, START + b * TILES + TILES)
                pe.wait_ge(bank_read, START + b * CHUNKS + c)
                if c == 0:
                    pe.wait_ge(y_down, START + b * TILES)
                product(ps[:, :], [(w[:, wp, k, c * P:(c + 1) * P], xT[:, xp, k, :])
                                   for k in range(KT) for xp, wp in TERMS], sem_done)

            def down(b, t):
                pe.wait_ge(hT_lo, START + (b + 1) * CHUNKS)
                if t >= 2:
                    pe.wait_ge(y_down, START + b * TILES + t - 1)
                else:
                    pe.wait_ge((inner_g, inner_gu)[t], START + (b + 1) * CHUNKS)
                product(ps_f[t % 2][:, :], [(hT[:, hp, c, t * P:(t + 1) * P], wd_s[:, wp, c, :])
                                            for c in range(CHUNKS) for hp, wp in TERMS], downed)

            def out(b, t):
                pe.wait_ge(aT_lo, START + (b + 1) * GROUPS)
                if t >= 2:
                    pe.wait_ge(y_done, START + b * TILES + t - 1)
                else:
                    pe.wait_ge((inv_back, attended)[t], START + (b + 1) * GROUPS)
                product((ps_t, ps_o)[t % 2][:, :], [(aT[:, ap, g, t * P:(t + 1) * P], wo_s[:, wp, g, :])
                                                    for g in range(GROUPS) for ap, wp in TERMS], outed)

            def steps(b, todo, first=False):
                nb = 0 if first else b + 1
                for s in todo:
                    if s[0] == "score":
                        score(b, s[1])
                    elif s[0] == "turn_p":
                        turn_p(b, s[1])
                    elif s[0] == "values":
                        values(b, s[1])
                    elif s[0] == "norm":
                        norm(b, s[1])
                    elif s[0] == "gate":
                        inner_half(b, s[1], wg_s, ps_f[0], inner_g, gated)
                    elif s[0] == "up":
                        inner_half(b, s[1], wu_s, ps_f[1], inner_gu, upped)
                    elif s[0] == "down":
                        down(b, s[1])
                    elif s[0] == "out":
                        out(b, s[1])
                    elif s[0] == "turn_x":
                        turn_x(nb, s[1], first)
                    elif s[0] == "project":
                        project(nb if s[1] == 0 else b, s[1], s[2], first)
                    elif s[0] == "turn_qk":
                        turn_qk(nb if s[1] == 0 else b, s[1], s[2])

            for own in (scored, p_turned, valued, inv_turned, projected, qk_turned, gated, upped, x_turned,
                        downed, outed):
                pe.sem_inc(own, START)
            pe.wait_ge(consts_done, 6)
            pe.wait_ge(w_lo, len(pieces))
            steps(0, head_steps(), first=True)
            with pe.Fori(0, BATCH - 1) as b:
                steps(b, main_steps())
                steps(b, tail_steps(True))
            steps(BATCH - 1, main_steps())
            steps(BATCH - 1, tail_steps(False))

        @block.vector
        def _(dve):
            def ln(b, t):
                at = b * TILES + t
                dve.wait_ge(x_loaded[t % 2], (b * (TILES // 2) + t // 2 + 1) * 16)
                nc.vector.bn_stats(stats[:, t % 2, :], x_in[:, t % 2, :]).then_inc(stats_done, 1)
                dve.wait_ge(stats_done, START + at + 1)
                dve.sem_inc(dve_passed, 1)
                nc.vector.bn_aggr(mean_var[:, t % 2, :], stats[:, t % 2, :]).then_inc(var_done, 1)
                dve.wait_ge(rstd_done, START + 2 * at + 2)
                nc.vector.tensor_scalar(x_in[:, t % 2, :], x_in[:, t % 2, :], mean_var[:, t % 2, 0:1],
                                        rstd[:, t % 2, 1:2], ALU.subtract, ALU.mult).then_inc(x_normed, 1)

            def turn_x(b, t):
                dve.wait_ge(xT_hi, START + b * TILES + t + 1)
                nc.vector.tensor_tensor(xT[:, LO, :, t * P:(t + 1) * P],
                                        ps_s[t % 2][:, :].rearrange("p (k q) -> p k q", k=KT),
                                        xT[:, HI, :, t * P:(t + 1) * P], ALU.subtract).then_inc(xT_lo, 1)

            def project(b, g, t):
                a = b * ROWS + g * TILES + t
                dve.wait_ge(projected, START + a + 1)
                dve.wait_ge(qk_summed, START + a)
                src = ps_a[:, 0:2 * P].rearrange("p (n d) -> p n d", d=HD)
                cos, sin = (rope_s[:, t, k, :][:, None, :].broadcast_to([P, 2 * GH, HD]) for k in range(2))
                nc.vector.tensor_tensor(x_cos[:, :].rearrange("p (n d) -> p n d", d=HD), src, cos,
                                        ALU.mult).then_inc(rotated, 1)
                swapped = ps_a[:, 0:2 * P].rearrange("p (n d two) -> p n d two", two=2, d=HD // 2)[:, :, :, ::-1]
                sin = rope_s[:, t, 1, :].rearrange("p (d two) -> p d two", two=2)[:, None, :, :].broadcast_to(
                    [P, 2 * GH, HD // 2, 2])
                nc.vector.tensor_tensor(x_sin[:, :].rearrange("p (n d two) -> p n d two", two=2, d=HD // 2), swapped,
                                        sin, ALU.mult).then_inc(rotated, 1)
                dve.wait_ge(v_hi, START + a + 1)
                nc.vector.scalar_tensor_tensor(v[:, g % 2, LO, t, :], ps_a[:, 2 * P:3 * P], QKV_OUT,
                                               v[:, g % 2, HI, t, :], ALU.mult, ALU.subtract).then_inc(v_lo, 1)

            def turn_qk(b, g, t):
                a = b * ROWS + g * TILES + t
                dve.wait_ge(qk_turned, START + a + 1)
                dve.wait_ge(scored, START + b * UNITS + (g - 1) * TILES * GH if g else b * UNITS)
                nc.vector.tensor_copy(qkT[:, g % 2, t, :, :, :].rearrange("p q h n -> p (q h n)"),
                                      ps_q[:, :]).then_inc(qkT_done, 1)

            def score(b, n):
                g, i, h = unit(n)
                width = (i + 1) * P
                dve.wait_ge(scored, START + b * UNITS + n + 1)
                dve.sem_inc(dve_passed, 1)
                nc.vector.tensor_tensor_reduce(
                    out=ps_s[n % 2][:, 0:width], in0=ps_s[n % 2][:, 0:width], in1=mask[:, SEQ - width:SEQ],
                    scale=-SCORE, scalar=3.0e38, op0=ALU.add, op1=ALU.min,
                    accum_out=neg_max[:, n % 4:n % 4 + 1]).then_inc(max_done, 1)

            def turn_p(b, n):
                g, i, h = unit(n)
                row, width = n // GH, (i + 1) * P
                dve.wait_ge(pT_hi, START + b * UNITS + n + 1)
                nc.vector.scalar_tensor_tensor(pT[:, row % 2, h, LO, 0:width], ps_t[:, 0:width], P_SCALE,
                                               pT[:, row % 2, h, HI, 0:width], ALU.mult,
                                               ALU.subtract).then_inc(pT_lo, 1)

            def row_sums(b, g):
                dve.wait_ge(exp_done, START + b * UNITS + (g + 1) * TILES * GH)
                dve.wait_ge(inv_spread, START + b * GROUPS + g)
                nc.vector.reciprocal(inv[:, :], sums[:, g % 2, :]).then_inc(inv_done, 1)

            def norm(b, g):
                dve.wait_ge(inv_back, START + b * GROUPS + g + 1)
                dve.wait_ge(valued, START + b * ROWS + (g + 1) * TILES)
                nc.vector.tensor_tensor(spread[:, :], ps_o[:, :], spread[:, :], ALU.mult).then_inc(attended, 1)

            def gate(b, c):
                dve.wait_ge(tanh_done, START + b * CHUNKS + c + 1)
                dve.wait_ge(hT_lo, START + b * CHUNKS + (c - 1 if c >= 2 else 0))
                nc.vector.scalar_tensor_tensor(inner[:, c % 2, :], tanh[:, :], 1.0, ps_f[0][:, :], ALU.add,
                                               ALU.mult).then_inc(inner_g, 1)

            def up(b, c):
                dve.wait_ge(inner_g, START + b * CHUNKS + c + 1)
                dve.wait_ge(upped, START + b * CHUNKS + c + 1)
                nc.vector.scalar_tensor_tensor(inner[:, c % 2, :], inner[:, c % 2, :], gate_up[:, c:c + 1],
                                               ps_f[1][:, :], ALU.mult, ALU.mult).then_inc(inner_gu, 1)

            def down(b, t):
                dve.wait_ge(downed, START + b * TILES + t + 1)
                if t == 0:
                    dve.wait_ge(valued, START + (b + 1) * ROWS)
                nc.vector.tensor_tensor(y[:, t, :], ps_f[t % 2][:, :], down_row[:, :], ALU.mult).then_inc(y_down, 1)

            def out(b, t):
                dve.wait_ge(outed, START + b * TILES + t + 1)
                dve.wait_ge(y_x, START + b * TILES + t + 1)
                nc.vector.scalar_tensor_tensor(y[:, t, :], (ps_t, ps_o)[t % 2][:, :], WO_OUT, y[:, t, :], ALU.mult,
                                               ALU.add).then_inc(y_done, 1)

            def steps(b, todo, first=False):
                nb = 0 if first else b + 1
                for s in todo:
                    if s[0] == "score":
                        score(b, s[1])
                    elif s[0] == "turn_p":
                        turn_p(b, s[1])
                    elif s[0] == "sums":
                        row_sums(b, s[1])
                    elif s[0] == "norm":
                        norm(b, s[1])
                    elif s[0] == "gate":
                        gate(b, s[1])
                    elif s[0] == "up":
                        up(b, s[1])
                    elif s[0] == "down":
                        down(b, s[1])
                    elif s[0] == "out":
                        out(b, s[1])
                    elif s[0] == "ln":
                        ln(nb, s[1])
                    elif s[0] == "turn_x":
                        turn_x(nb, s[1])
                    elif s[0] == "project":
                        project(nb if s[1] == 0 else b, s[1], s[2])
                    elif s[0] == "turn_qk":
                        turn_qk(nb if s[1] == 0 else b, s[1], s[2])

            for own in (stats_done, var_done, x_normed, xT_lo, rotated, v_lo, qkT_done, max_done, pT_lo,
                        inv_done, attended, inner_g, inner_gu, y_down, y_done):
                dve.sem_inc(own, START)
            dve.wait_ge(consts_loaded, 64)
            nc.vector.scalar_tensor_tensor(gate_up[:, :], gate_up[:, :], 0.5 * G_OUT * G_OUT * H_SCALE,
                                           gate_half[:, :], ALU.mult, ALU.mult).then_inc(scales_done, 1)
            nc.vector.tensor_scalar(down_row[:, :], down_row[:, :], D_OUT, None, ALU.mult).then_inc(scales_done, 1)
            dve.wait_ge(scales_done, 1)
            nc.vector.tensor_scalar(gate_half[:, :], gate_half[:, :], 0.5 * G_OUT, None,
                                    ALU.mult).then_inc(scales_done, 1)
            for k, (src, dst, scale, at, width) in enumerate(pieces):
                dve.wait_ge(w_hi, k + 1)
                nc.vector.scalar_tensor_tensor(flat(dst, LO)[:, at:at + width], staging[:, k % 2, 0:width], scale,
                                               flat(dst, HI)[:, at:at + width], ALU.mult,
                                               ALU.subtract).then_inc(w_lo, 1)
            dve.wait_ge(scales_done, 3)
            steps(0, head_steps(), first=True)
            with dve.Fori(0, BATCH - 1) as b:
                steps(b, main_steps())
                steps(b, tail_steps(True))
            steps(BATCH - 1, main_steps())
            steps(BATCH - 1, tail_steps(False))

        @block.scalar
        def _(act):
            def turn_x(b, t):
                act.wait_ge(x_turned, START + b * TILES + t + 1)
                if t == 0:
                    act.wait_ge(upped, START + b * CHUNKS)
                    act.wait_ge(projected, START + b * ROWS)
                nc.scalar.activation(xT[:, HI, :, t * P:(t + 1) * P],
                                     ps_s[t % 2][:, :].rearrange("p (k q) -> p k q", k=KT),
                                     ACT.Copy).then_inc(xT_hi, 1)

            def project(b, g, t):
                a = b * ROWS + g * TILES + t
                act.wait_ge(rotated, START + 2 * a + 2)
                if t == 0:
                    act.wait_ge(valued, START + b * ROWS + (g - 1) * TILES if g else b * ROWS)
                nc.scalar.activation(v[:, g % 2, HI, t, :], ps_a[:, 2 * P:3 * P], ACT.Copy,
                                     scale=QKV_OUT).then_inc(v_hi, 1)

            def split_qk(b, g, t, first=False):
                a = b * ROWS + g * TILES + t
                act.wait_ge(qk_summed, START + a + 1)
                if not (first and t < 2):
                    act.wait_ge(qk_turned, START + a - 1)
                for q in range(2):
                    src = qk[:, t % 2, q * P:(q + 1) * P].rearrange("p (h d) -> p h d", h=GH)
                    parts = qk_parts[:, t % 2, q, :, :, :]
                    parts = parts[:, :, 0:2, :] if q == 0 else parts[:, :, 0:4:2, :]
                    nc.scalar.activation(parts, src[:, :, None, :].broadcast_to([P, GH, 2, HD]),
                                         ACT.Copy).then_inc(qk_hi, 1)

            def score(b, n):
                g, i, h = unit(n)
                width = (i + 1) * P
                act.wait_ge(max_done, START + b * UNITS + n + 1)
                act.wait_ge(p_turned, START + b * UNITS + (n - 1 if n >= 2 else 0))
                if n % (TILES * GH) == 0:
                    act.wait_ge(inv_done, START + b * GROUPS + (g - 1 if g else 0))
                nc.scalar.activation(probs[:, n % 2, 0:width], ps_s[n % 2][:, 0:width], ACT.Exp,
                                     bias=neg_max[:, n % 4:n % 4 + 1], scale=-1.0,
                                     accum_out=sums[:, g % 2, i * GH + h:i * GH + h + 1]).then_inc(exp_done, 1)

            def turn_p(b, n):
                g, i, h = unit(n)
                row, width = n // GH, (i + 1) * P
                act.wait_ge(p_turned, START + b * UNITS + n + 1)
                if h == 0:
                    act.wait_ge(valued, START + b * ROWS + (row - 1 if row else 0))
                if n == 0:
                    act.wait_ge(stored, START + 16 * TILES * b)
                nc.scalar.activation(pT[:, row % 2, h, HI, 0:width], ps_t[:, 0:width], ACT.Copy,
                                     scale=P_SCALE).then_inc(pT_hi, 1)

            def norm(b, g):
                act.wait_ge(inv_turned, START + b * GROUPS + g + 1)
                nc.scalar.activation(spread[:, :], ps_t[:, :], ACT.Copy).then_inc(inv_back, 1)
                act.wait_ge(attended, START + b * GROUPS + g + 1)
                if g == 0:
                    act.wait_ge(outed, START + b * TILES)
                nc.scalar.activation(aT[:, HI, g, :], spread[:, :], ACT.Copy).then_inc(aT_hi, 1)

            def gate(b, c):
                act.wait_ge(gated, START + b * CHUNKS + c + 1)
                act.wait_ge(inner_g, START + b * CHUNKS + c)
                nc.scalar.activation(tanh[:, :], ps_f[0][:, :], ACT.Tanh,
                                     scale=gate_half[:, c:c + 1]).then_inc(tanh_done, 1)

            def split_h(b, c):
                act.wait_ge(inner_gu, START + b * CHUNKS + c + 1)
                if c == 0:
                    act.wait_ge(downed, START + b * TILES)
                nc.scalar.activation(hT[:, HI, c, :], inner[:, c % 2, :], ACT.Copy).then_inc(hT_hi, 1)

            def steps(b, todo, first=False):
                nb = 0 if first else b + 1
                for s in todo:
                    if s[0] == "score":
                        score(b, s[1])
                    elif s[0] == "turn_p":
                        turn_p(b, s[1])
                    elif s[0] == "norm":
                        norm(b, s[1])
                    elif s[0] == "gate":
                        gate(b, s[1])
                    elif s[0] == "split_h":
                        split_h(b, s[1])
                    elif s[0] == "turn_x":
                        turn_x(nb, s[1])
                    elif s[0] == "project":
                        project(nb if s[1] == 0 else b, s[1], s[2])
                    elif s[0] == "split_qk":
                        split_qk(nb if s[1] == 0 else b, s[1], s[2], first)

            for own in (xT_hi, v_hi, qk_hi, exp_done, pT_hi, inv_back, aT_hi, tanh_done, hT_hi):
                act.sem_inc(own, START)
            for k, (src, dst, scale, at, width) in enumerate(pieces):
                act.wait_ge(w_loaded[k % 2], 16 * (k // 2 + 1))
                nc.scalar.activation(flat(dst, HI)[:, at:at + width], staging[:, k % 2, 0:width], ACT.Copy,
                                     scale=scale).then_inc(w_hi, 1)
            act.wait_ge(scales_done, 3)
            act.wait_ge(w_lo, len(pieces))
            steps(0, head_steps(), first=True)
            with act.Fori(0, BATCH - 1) as b:
                steps(b, main_steps())
                steps(b, tail_steps(True))
            steps(BATCH - 1, main_steps())
            steps(BATCH - 1, tail_steps(False))

        @block.gpsimd
        def _(pool):
            def ln(b, t, first=False):
                at = b * TILES + t
                pool.wait_ge(var_done, START + at + 1)
                if not (first and t < 2):
                    pool.wait_ge(x_normed, START + at - 1)
                pool.sem_inc(pool_passed, 1)
                nc.gpsimd.tensor_scalar(rstd[:, t % 2, 0:1], mean_var[:, t % 2, 1:2], EPS, X_SCALE ** -2, ALU.add,
                                        ALU.mult).then_inc(rstd_done, 1)
                pool.wait_ge(rstd_done, START + 2 * at + 1)
                nc.gpsimd.tensor_tensor(rstd[:, t % 2, 1:2], rstd[:, t % 2, 0:1], neg_half[:, :],
                                        ALU.pow).then_inc(rstd_done, 1)

            def project(b, g, t, first=False):
                a = b * ROWS + g * TILES + t
                pool.wait_ge(rotated, START + 2 * a + 2)
                if not (first and t < 2):
                    pool.wait_ge(qk_lo, START + 2 * a - 2)
                nc.gpsimd.tensor_tensor(qk[:, t % 2, :], x_cos[:, :], x_sin[:, :], ALU.add).then_inc(qk_summed, 1)

            def split_qk(b, g, t):
                a = b * ROWS + g * TILES + t
                for q in range(2):
                    pool.wait_ge(qk_hi, START + 2 * a + q + 1)
                    src = qk[:, t % 2, q * P:(q + 1) * P].rearrange("p (h d) -> p h d", h=GH)
                    parts = qk_parts[:, t % 2, q, :, :, :]
                    hi, lo = (parts[:, :, 0:2, :], parts[:, :, 2:4, :]) if q == 0 else (parts[:, :, 0:4:2, :],
                                                                                      parts[:, :, 1:4:2, :])
                    nc.gpsimd.tensor_tensor(lo, src[:, :, None, :].broadcast_to([P, GH, 2, HD]), hi,
                                            ALU.subtract).then_inc(qk_lo, 1)

            def row_sums(b, g):
                pool.wait_ge(inv_done, START + b * GROUPS + g + 1)
                pool.wait_ge(aT_lo, START + b * GROUPS + g)
                pool.sem_inc(pool_passed, 1)
                nc.gpsimd.tensor_scalar(spread[:, :].rearrange("p (n d) -> p n d", d=HD),
                                        inv[:, :][:, :, None].broadcast_to([P, TILES * GH, HD]), A_OUT, 1.0,
                                        ALU.mult, ALU.mult).then_inc(inv_spread, 1)

            def norm(b, g):
                pool.wait_ge(aT_hi, START + b * GROUPS + g + 1)
                nc.gpsimd.tensor_tensor(aT[:, LO, g, :], spread[:, :], aT[:, HI, g, :],
                                        ALU.subtract).then_inc(aT_lo, 1)

            def split_h(b, c):
                pool.wait_ge(hT_hi, START + b * CHUNKS + c + 1)
                nc.gpsimd.tensor_tensor(hT[:, LO, c, :], inner[:, c % 2, :], hT[:, HI, c, :],
                                        ALU.subtract).then_inc(hT_lo, 1)

            def down(b, t):
                pool.wait_ge(y_down, START + b * TILES + t + 1)
                pool.wait_ge(res_loaded[t % 2], (b * (TILES // 2) + t // 2 + 1) * 16)
                nc.gpsimd.tensor_tensor(y[:, t, :], y[:, t, :], x_res[:, t % 2, :], ALU.add).then_inc(y_x, 1)

            def steps(b, todo, first=False):
                nb = 0 if first else b + 1
                for s in todo:
                    if s[0] == "sums":
                        row_sums(b, s[1])
                    elif s[0] == "norm":
                        norm(b, s[1])
                    elif s[0] == "split_h":
                        split_h(b, s[1])
                    elif s[0] == "down":
                        down(b, s[1])
                    elif s[0] == "ln":
                        ln(nb, s[1], first)
                    elif s[0] == "project":
                        project(nb if s[1] == 0 else b, s[1], s[2], first)
                    elif s[0] == "split_qk":
                        split_qk(nb if s[1] == 0 else b, s[1], s[2])

            for own in (rstd_done, qk_summed, qk_lo, inv_spread, aT_lo, hT_lo, y_x):
                pool.sem_inc(own, START)
            nc.gpsimd.memset(ident[:, :], 0.0).then_inc(consts_done, 1)
            nc.gpsimd.memset(mask[:, :], 0.0).then_inc(consts_done, 1)
            nc.gpsimd.memset(neg_half[:, :], -0.5).then_inc(consts_done, 1)
            pool.wait_ge(consts_done, 3)
            nc.gpsimd.affine_select(out=ident[:, :], in_=ident[:, :], compare_op=ALU.not_equal, fill=1.0, base=0,
                                    pattern=[[-1, P]], channel_multiplier=1).then_inc(consts_done, 1)
            nc.gpsimd.affine_select(out=mask[:, SEQ - P:SEQ], in_=mask[:, SEQ - P:SEQ], compare_op=ALU.is_ge,
                                    fill=MASKED, base=0, pattern=[[-1, P]],
                                    channel_multiplier=1).then_inc(consts_done, 1)
            pool.wait_ge(consts_done, 4)
            nc.gpsimd.tensor_copy(ident16[:, :], ident[:, :]).then_inc(consts_done, 1)
            steps(0, head_steps(), first=True)
            with pool.Fori(0, BATCH - 1) as b:
                steps(b, main_steps())
                steps(b, tail_steps(True))
            steps(BATCH - 1, main_steps())
            steps(BATCH - 1, tail_steps(False))


def rope_table():
    freqs = np.exp(np.float32(-np.log(10000.0)) * np.arange(0, HD, 2, dtype=np.float32) / np.float32(HD))
    angles = np.arange(SEQ, dtype=np.float32)[:, None] * freqs.astype(np.float32)[None, :]
    cos = np.repeat(np.cos(angles), 2, axis=-1)
    sin = np.repeat(np.sin(angles), 2, axis=-1) * np.tile(np.float32([-1, 1]), HD // 2)
    table = np.stack([cos, sin], axis=1).astype(np.float32) * np.float32(QKV_OUT)
    return np.ascontiguousarray(table.reshape(TILES, P, 2, HD).transpose(1, 0, 2, 3))


def kernel(L0_attn_x, L0_attn_Wqkv, L0_attn_WO, L0_ffn_gate_w, L0_ffn_up_w, L0_ffn_down_w, L0_ffn_gate_s,
           L0_ffn_up_s, L0_ffn_down_s):
    import concourse.bacc as bacc
    from concourse.bass_utils import run_bass_kernel_spmd

    def by_partition(w):
        rows, cols = w.shape
        return np.ascontiguousarray(w.reshape(rows // P, P, cols).transpose(1, 0, 2).reshape(P, -1))

    qkv = np.asarray(L0_attn_Wqkv).T.reshape(DIM, 3, GROUPS, P).transpose(0, 2, 1, 3).reshape(DIM, 3 * DIM)
    arrays = {
        "x": np.ascontiguousarray(L0_attn_x),
        "wqkv": by_partition(qkv),
        "wo": by_partition(np.asarray(L0_attn_WO).T),
        "wg": by_partition(np.asarray(L0_ffn_gate_w).T),
        "wu": by_partition(np.asarray(L0_ffn_up_w).T),
        "wd": by_partition(np.asarray(L0_ffn_down_w).T),
        "gate_s": np.ascontiguousarray(np.asarray(L0_ffn_gate_s).reshape(CHUNKS, P).T),
        "up_s": np.ascontiguousarray(np.asarray(L0_ffn_up_s).reshape(CHUNKS, P).T),
        "down_s": np.ascontiguousarray(np.asarray(L0_ffn_down_s).reshape(1, DIM)),
        "rope": rope_table(),
    }
    nc = bacc.Bacc("TRN2", target_bir_lowering=False, num_devices=1)
    args = [nc.dram_tensor(f"{k}_dram", a.shape, mybir.dt.from_np(a.dtype), kind="ExternalInput").ap()
            for k, a in arrays.items()]
    y = nc.dram_tensor("y_dram", (BATCH, SEQ, DIM), F32, kind="ExternalOutput").ap()
    layer(nc, *args, y)
    r = run_bass_kernel_spmd(nc, [{f"{k}_dram": a for k, a in arrays.items()}], core_ids=[0])
    return r.results[0]["y_dram"]
```

```python
from contextlib import ExitStack

import numpy as np

import concourse.bass as bass

from concourse import mybir

F32 = mybir.dt.float32
F16 = mybir.dt.float16
BF16 = mybir.dt.bfloat16
ALU = mybir.AluOpType
ACT = mybir.ActivationFunctionType

P = 128
BATCH, SEQ, DIM = 8, 512, 512
HEADS, HD = 16, 32
INNER = 1408
TILES = SEQ // P
KT = DIM // P
GROUPS = HEADS * HD // P
GH = P // HD
CHUNKS = INNER // P
ROWS = GROUPS * TILES
UNITS = ROWS * GH
EPS = 1e-5
HI, LO = 0, 1
TERMS = ((HI, HI), (LO, HI), (HI, LO))

X_SCALE = 2.0 ** 8
W_SCALE = 2.0 ** 10
F_SCALE = 2.0 ** 6
QKV_SCALE = 2.0 ** 6
P_SCALE = 2.0 ** 10
A_SCALE = 2.0 ** 8
H_SCALE = 2.0 ** 4
QKV_OUT = QKV_SCALE / (X_SCALE * W_SCALE)
SCORE = HD ** -0.5 / QKV_SCALE ** 2
A_OUT = A_SCALE / (P_SCALE * QKV_SCALE)
WO_OUT = 1.0 / (A_SCALE * W_SCALE)
G_OUT = 1.0 / (X_SCALE * F_SCALE)
D_OUT = 1.0 / (H_SCALE * F_SCALE)
MASKED = -1e30
PROJECT_COST, TURN_COST, INNER_COST = 0.48, 0.5, 0.43
START = 1


def main_steps():
    a_tiles = [(1 + r // TILES, r % TILES) for r in range((GROUPS - 1) * TILES)]
    inner = [(kind, c, part) for c in range(CHUNKS) for kind in ("gate", "up") for part in range(KT)]
    share = (len(a_tiles) * (KT * PROJECT_COST + TURN_COST) + len(inner) * INNER_COST) / UNITS
    out, later, spent = [("score", 0), ("exp", 0)], {}, 0.0
    for n in range(UNITS):
        row, at = divmod(n, GH)
        if n + 1 < UNITS:
            out.append(("score", n + 1))
        out += [("take_qk", *a_tiles[r]) for r in range(len(a_tiles)) if n == turn_qk_at(r) + 1]
        if n:
            out.append(("take_p", n - 1))
        if n + 1 < UNITS:
            out.append(("exp", n + 1))
        parts = ((0, 1), (2,), (3,), ())[at] if row < len(a_tiles) else ()
        spent += PROJECT_COST * len(parts)
        while inner and (spent + INNER_COST / 2 < share * (n + 1) or n == UNITS - 1):
            s = inner.pop(0)
            out.append(s)
            spent += INNER_COST
            if s[2] == KT - 1:
                later.setdefault(n + 1, []).append((f"times_{s[0]}", s[1]))
                if s[0] == "up":
                    later.setdefault(n + 2, []).append(("split_h", s[1]))
        if parts:
            out += [("project", *a_tiles[row], part) for part in parts]
            if parts == (3,):
                later.setdefault(n + 1, []).append(("take_v", *a_tiles[row]))
                later.setdefault(n + 1, []).append(("split_qk", *a_tiles[row]))
        for r in range(len(a_tiles)):
            if n == turn_qk_at(r):
                out.append(("turn_qk", *a_tiles[r]))
                spent += TURN_COST
        out.append(("turn_p", n))
        out += later.pop(n, [])
        if n % (GH * TILES) == GH * TILES - 1:
            out.append(("sums", n // (GH * TILES)))
        if at == 1 and row:
            out.append(("values", row - 1))
            if row % TILES == 0:
                out.append(("turn_inv", row // TILES - 1))
                later.setdefault(n + 1, []).insert(0, ("norm", row // TILES - 1))
                later.setdefault(n + 2, []).insert(0, ("take_a", row // TILES - 1))
    for n in sorted(later):
        out += later[n]
    return out + [("take_p", UNITS - 1)]


def turn_qk_at(r):
    return GH * r + 6


def tail_steps(more):
    a = [("ln", 0), ("ln", 1), ("down", 0), ("turn_x", 0), ("values", ROWS - 1), ("turn_inv", GROUPS - 1),
         ("turn_x", 1), ("norm", GROUPS - 1), ("ln", 2), ("take_a", GROUPS - 1), ("ln", 3), ("down", 1), ("turn_x", 2), ("turn_x", 3),
         ("project", 0, 0), ("down", 2), ("project", 0, 1), ("split_qk", 0, 0), ("down", 3), ("turn_qk", 0, 0),
         ("project", 0, 2), ("split_qk", 0, 1), ("take_qk", 0, 0), ("out", 0), ("turn_qk", 0, 1), ("project", 0, 3),
         ("split_qk", 0, 2), ("take_qk", 0, 1), ("out", 1), ("turn_qk", 0, 2), ("split_qk", 0, 3), ("take_qk", 0, 2),
         ("out", 2), ("turn_qk", 0, 3), ("take_qk", 0, 3), ("out", 3)]
    return whole(a if more else [s for s in a if s[0] in ("down", "out", "norm", "take_a", "turn_inv", "values")])


def head_steps():
    out = [("ln", 0), ("ln", 1), ("turn_x", 0), ("ln", 2), ("turn_x", 1), ("ln", 3), ("turn_x", 2), ("turn_x", 3)]
    for t in range(TILES):
        out += [("project", 0, t), ("split_qk", 0, t), ("turn_qk", 0, t), ("take_qk", 0, t)]
    return whole(out)


def whole(steps):
    return [x for s in steps for x in ([(*s, part) for part in range(KT)] + [("take_v", *s[1:])]
                                       if s[0] == "project" else [s])]


def unit(n):
    return n // (TILES * GH), n // GH % TILES, n % GH


def layer(nc, x, wqkv, wo, wg, wu, wd, gate_s, up_s, down_s, rope, y_out):
    ctx = ExitStack()
    with ctx:
        def sb(name, shape, dtype):
            return ctx.enter_context(nc.sbuf_tensor(name, shape, dtype))

        def pb(name, shape, dtype):
            return ctx.enter_context(nc.psum_tensor(name, shape, dtype))

        def sem(name):
            return ctx.enter_context(nc.semaphore(name))

        wqkv_s = sb("wqkv_s", [P, 2, KT, GROUPS * 3 * P], F16)
        wo_s = sb("wo_s", [P, 2, GROUPS, DIM], F16)
        wg_s = sb("wg_s", [P, 2, KT, INNER], F16)
        wu_s = sb("wu_s", [P, 2, KT, INNER], F16)
        wd_s = sb("wd_s", [P, 2, CHUNKS, DIM], F16)
        ident = sb("ident", [P, P], F32)
        ident16 = sb("ident16", [P, P], F16)
        mask = sb("mask", [P, SEQ], BF16)
        rope_s = sb("rope_s", [P, TILES, 2, HD], F32)
        down_row = sb("down_row", [P, DIM], F32)
        gate_half = sb("gate_half", [P, CHUNKS], F32)
        gate_up = sb("gate_up", [P, CHUNKS], F32)
        neg_half = sb("neg_half", [P, 1], F32)
        lo_max = sb("lo_max", [P, 6], F32)
        lo_most = sb("lo_most", [P, 2], F32)
        lo_any = sb("lo_any", [P, 1], mybir.dt.int32)
        x_in = sb("x_in", [P, 2, DIM], F32)
        stats = sb("stats", [P, 2, 6], F32)
        mean_var = sb("mean_var", [P, 2, 2], F32)
        rstd = sb("rstd", [P, 2, 2], F32)
        xT = sb("xT", [P, 2, KT, SEQ], F16)
        x_cos = sb("x_cos", [P, 2 * P], F32)
        x_sin = sb("x_sin", [P, 2 * P], F32)
        qk = sb("qk", [P, 2, 2 * P], F32)
        qk_parts = sb("qk_parts", [P, 2, 2, GH, 4, HD], F16)
        qkT = sb("qkT", [P, 2, TILES, 2, GH, P], F16)
        v = sb("v", [P, 2, 2, TILES, P], F16)
        neg_max = sb("neg_max", [P, 4], F32)
        probs = sb("probs", [P, 2, SEQ], F32)
        pT = sb("pT", [P, 2, GH, 2, SEQ], F16)
        sums = sb("sums", [P, 2, TILES * GH], F32)
        inv = sb("inv", [P, TILES * GH], F32)
        spread = sb("spread", [P, SEQ], F32)
        aT = sb("aT", [P, 2, GROUPS, SEQ], F16)
        tanh = sb("tanh", [P, SEQ], F32)
        inner = sb("inner", [P, 2, SEQ], F32)
        hT = sb("hT", [P, 2, CHUNKS, SEQ], F16)
        x_res = sb("x_res", [P, 2, DIM], F32)
        y = pT[:, 0, :, :, :].rearrange("p h s q -> p (h s q)").bitcast(F32).rearrange("p (t d) -> p t d", t=TILES)
        staging = hT[:, :, :, :].rearrange("p s c q -> p (s c q)").bitcast(F32).rearrange("p (r w) -> p r w", r=2)

        ps_s = [pb("ps_s0", [P, 512], F32), pb("ps_s1", [P, 512], F32)]
        ps_t = [pb("ps_t0", [P, 512], F32), pb("ps_t1", [P, 512], F32)]
        ps_o = pb("ps_o", [P, 512], F32)
        ps_a = pb("ps_a", [P, 512], F32)
        ps_f = [pb("ps_f0", [P, 512], F32), pb("ps_f1", [P, 512], F32)]

        consts_loaded = sem("consts_loaded")
        consts_done = sem("consts_done")
        scales_done = sem("scales_done")
        w_loaded = [sem("w_loaded0"), sem("w_loaded1")]
        w_hi = sem("w_hi")
        w_lo = sem("w_lo")
        lo_maxed = sem("lo_maxed")
        lo_gathered = sem("lo_gathered")
        lo_known = sem("lo_known")
        x_loaded = [sem("x_loaded0"), sem("x_loaded1")]
        res_loaded = [sem("res_loaded0"), sem("res_loaded1")]
        stored = sem("stored")
        scored = sem("scored")
        p_turned = sem("p_turned")
        valued = sem("valued")
        inv_turned = sem("inv_turned")
        projected = sem("projected")
        qk_turned = sem("qk_turned")
        gated = sem("gated")
        upped = sem("upped")
        x_turned = sem("x_turned")
        downed = sem("downed")
        outed = sem("outed")
        stats_done = sem("stats_done")
        var_done = sem("var_done")
        x_normed = sem("x_normed")
        xT_lo = sem("xT_lo")
        rotated = sem("rotated")
        v_lo = sem("v_lo")
        qkT_done = sem("qkT_done")
        max_done = sem("max_done")
        pT_lo = sem("pT_lo")
        inv_done = sem("inv_done")
        attended = sem("attended")
        inner_g = sem("inner_g")
        inner_gu = sem("inner_gu")
        y_down = sem("y_down")
        y_done = sem("y_done")
        xT_hi = sem("xT_hi")
        v_hi = sem("v_hi")
        qk_hi = sem("qk_hi")
        exp_done = sem("exp_done")
        pT_hi = sem("pT_hi")
        inv_back = sem("inv_back")
        aT_hi = sem("aT_hi")
        tanh_done = sem("tanh_done")
        hT_hi = sem("hT_hi")
        rstd_done = sem("rstd_done")
        qk_summed = sem("qk_summed")
        qk_lo = sem("qk_lo")
        inv_spread = sem("inv_spread")
        aT_lo = sem("aT_lo")
        hT_lo = sem("hT_lo")
        y_x = sem("y_x")

        dve_passed = sem("dve_passed")
        pool_passed = sem("pool_passed")

        def flat(w, part):
            return w[:, part, :, :].rearrange("p a n -> p (a n)")

        def inv_bank(g):
            return 0

        pieces = []
        for src, dst, scale, cut in ((wqkv, wqkv_s, W_SCALE, 3), (wo, wo_s, W_SCALE, 1), (wg, wg_s, F_SCALE, 2),
                                     (wu, wu_s, F_SCALE, 2), (wd, wd_s, F_SCALE, 2)):
            width = src.shape[1] // cut
            pieces += [(src, dst, scale, k * width, width) for k in range(cut)]

        first_inner = next(k for k, piece in enumerate(pieces) if piece[0] is wg)
        inner_pieces = len(pieces) - first_inner

        x_v = x.rearrange("b (t p) d -> b p t d", p=P)
        y_v = y_out.rearrange("b (t p) d -> b p t d", p=P)

        block = ctx.enter_context(nc.Block())

        @block.sync
        def _(sp):
            def load_x(b, t, wait=True):
                if wait:
                    sp.wait_ge(x_turned, START + b * TILES + t - 1)
                sp.dma_start(x_in[:, t % 2, :], x_v[b][:, t, :]).then_inc(x_loaded[t % 2], 16)

            def load_res(b, t):
                sp.wait_ge(y_x, START + b * TILES + (t - 1 if t >= 2 else 0))
                sp.dma_start(x_res[:, t % 2, :], x_v[b][:, t, :]).then_inc(res_loaded[t % 2], 16)

            def steps(b, todo):
                for s in todo:
                    if s == ("turn_x", 0) or s == ("turn_x", 1):
                        load_x(b + 1, s[1] + 2)
                    elif s == ("down", 0) or s == ("down", 1):
                        load_res(b, s[1] + 2)
                    elif s[0] == "out":
                        t = s[1]
                        sp.wait_ge(y_done, START + b * TILES + t + 1)
                        sp.dma_start(y_v[b][:, t, :], y[:, t, :]).then_inc(stored, 16)

            sp.sem_inc(stored, START)
            load_x(0, 0, wait=False)
            load_x(0, 1, wait=False)
            sp.dma_start(rope_s[:, :, :, :], rope).then_inc(consts_loaded, 16)
            sp.dma_start(gate_half[:, :], gate_s).then_inc(consts_loaded, 16)
            sp.dma_start(gate_up[:, :], up_s).then_inc(consts_loaded, 16)
            sp.dma_start(down_row[:, :], down_s.broadcast_to([P, DIM])).then_inc(consts_loaded, 16)
            for k, (src, dst, scale, at, width) in enumerate(pieces):
                if k >= 2:
                    sp.wait_ge(w_lo, k - 1)
                sp.dma_start(staging[:, k % 2, 0:width], src[:, at:at + width]).then_inc(w_loaded[k % 2], 16)
            load_x(0, 2)
            load_x(0, 3)
            with sp.Fori(0, BATCH - 1) as b:
                load_res(b, 0)
                load_res(b, 1)
                load_x(b + 1, 0)
                load_x(b + 1, 1)
                steps(b, tail_steps(True))
            load_res(BATCH - 1, 0)
            load_res(BATCH - 1, 1)
            steps(BATCH - 1, tail_steps(False))
            sp.wait_ge(stored, START + 16 * BATCH * TILES)

        @block.tensor
        def _(pe):
            def product(ps, pairs, sem_done):
                for k, (stationary, moving) in enumerate(pairs):
                    last = nc.tensor.matmul(ps, stationary, moving, start=(k == 0), stop=(k == len(pairs) - 1))
                last.then_inc(sem_done, 1)

            def turn_x(b, t, first=False):
                pe.wait_ge(x_normed, START + b * TILES + t + 1)
                if t >= 2:
                    pe.wait_ge(xT_lo, START + b * TILES + t - 1)
                elif not first:
                    pe.wait_ge(exp_done, START + (b - 1) * UNITS + UNITS - 1 + t)
                for k in range(KT):
                    last = nc.tensor.transpose(ps_s[t % 2][:, k * P:(k + 1) * P], x_in[:, t % 2, k * P:(k + 1) * P],
                                               ident[:, :])
                last.then_inc(x_turned, 1)

            def project(b, g, t, k, first=False):
                a = b * ROWS + g * TILES + t
                if k == 0:
                    pe.wait_ge(xT_lo, START + b * TILES + t + 1)
                    if not (first and t == 0):
                        pe.wait_ge(v_lo, START + a)
                for xp, wp in TERMS:
                    last = nc.tensor.matmul(ps_a[:, 0:3 * P], xT[:, xp, k, t * P:(t + 1) * P],
                                            wqkv_s[:, wp, k, g * 3 * P:(g + 1) * 3 * P],
                                            start=(k == 0 and (xp, wp) == TERMS[0]),
                                            stop=(k == KT - 1 and (xp, wp) == TERMS[-1]))
                if k == KT - 1:
                    last.then_inc(projected, 1)

            def turn_qk(b, g, t):
                a = b * ROWS + g * TILES + t
                pe.wait_ge(qk_lo, START + 2 * a + 2)
                if g:
                    n = turn_qk_at((g - 1) * TILES + t)
                    pe.wait_ge(pT_lo, START + b * UNITS + n)
                elif t:
                    n = 0
                    pe.wait_ge(qkT_done, START + a)
                else:
                    n = 0
                    pe.wait_ge(pT_lo, START + b * UNITS)
                into = ps_t[(n + 1) % 2][:, :].bitcast(F16)
                for q in range(2):
                    for h in range(GH):
                        last = nc.tensor.transpose(
                            into[:, (q * GH + h) * P:(q * GH + h + 1) * P],
                            qk_parts[:, t % 2, q, h, :, :].rearrange("p s d -> p (s d)"), ident16[:, :])
                last.then_inc(qk_turned, 1)

            def score(b, n):
                g, i, h = unit(n)
                pe.wait_ge(qkT_done, START + b * ROWS + n // GH + 1)
                if n < 2:
                    pe.wait_ge(xT_lo, START + b * TILES + TILES)
                else:
                    pe.wait_ge(exp_done, START + b * UNITS + n - 1)
                nc.tensor.matmul(ps_s[n % 2][:, 0:(i + 1) * P], qkT[:, g % 2, i, 0, h, :],
                                 qkT[:, g % 2, 0:i + 1, 1, h, :], start=True, stop=True).then_inc(scored, 1)

            def turn_p(b, n):
                g, i, h = unit(n)
                pe.wait_ge(exp_done, START + b * UNITS + n + 1)
                if n == 0:
                    pe.wait_ge(y_done, START + b * TILES)
                elif n == 1:
                    pe.wait_ge(qkT_done, START + b * ROWS + TILES)
                else:
                    pe.wait_ge(pT_lo, START + b * UNITS + n - 1)
                if n > TILES * GH and n % (TILES * GH) == 2:
                    pe.wait_ge(inv_back, START + b * GROUPS + g)
                r = (n - 1 - turn_qk_at(0)) // GH
                if n - 1 == turn_qk_at(r) and 0 <= r < (GROUPS - 1) * TILES:
                    pe.wait_ge(qkT_done, START + b * ROWS + TILES + r + 1)
                for j in range(i + 1):
                    last = nc.tensor.transpose(ps_t[n % 2][:, j * P:(j + 1) * P], probs[:, n % 2, j * P:(j + 1) * P],
                                               ident[:, :])
                last.then_inc(p_turned, 1)

            def values(b, row):
                g, i = divmod(row, TILES)
                pe.wait_ge(pT_lo, START + b * UNITS + (row + 1) * GH)
                pe.wait_ge(v_lo, START + b * ROWS + row + 1)
                if i == 0:
                    pe.wait_ge(attended, START + b * GROUPS + g)
                    pe.wait_ge(y_done, START + b * TILES)
                for j in range(i + 1):
                    for k, (pp, vp) in enumerate(TERMS):
                        for h in range(GH):
                            last = nc.tensor.matmul(
                                ps_o[h * HD:(h + 1) * HD, i * P:(i + 1) * P], v[:, g % 2, vp, j, h * HD:(h + 1) * HD],
                                pT[:, row % 2, h, pp, j * P:(j + 1) * P],
                                start=(j == 0 and k == 0), stop=(j == i and k == len(TERMS) - 1))
                last.then_inc(valued, 1)

            def turn_inv(b, g):
                pe.wait_ge(inv_spread, START + b * GROUPS + g + 1)
                n = min((g + 1) * TILES * GH + 1, UNITS - 1)
                pe.wait_ge(pT_lo, START + b * UNITS + n)
                for i in range(TILES):
                    last = nc.tensor.transpose(ps_t[inv_bank(g)][:, i * P:(i + 1) * P], spread[:, i * P:(i + 1) * P],
                                               ident[:, :])
                last.then_inc(inv_turned, 1)

            def inner_part(b, c, k, w, ps, bank_read, sem_done, inner_terms):
                if k == 0:
                    pe.wait_ge(xT_lo, START + b * TILES + TILES)
                    pe.wait_ge(bank_read, START + b * CHUNKS + c)
                    if c == 0:
                        pe.wait_ge(y_down, START + b * TILES)
                for xp, wp in inner_terms:
                    last = nc.tensor.matmul(ps[:, :], w[:, wp, k, c * P:(c + 1) * P], xT[:, xp, k, :],
                                            start=(k == 0 and (xp, wp) == inner_terms[0]),
                                            stop=(k == KT - 1 and (xp, wp) == inner_terms[-1]))
                if k == KT - 1:
                    last.then_inc(sem_done, 1)

            def down(b, t, inner_terms):
                pe.wait_ge(hT_lo, START + (b + 1) * CHUNKS)
                if t >= 2:
                    pe.wait_ge(y_down, START + b * TILES + t - 1)
                else:
                    pe.wait_ge((inner_g, inner_gu)[t], START + (b + 1) * CHUNKS)
                product(ps_f[t % 2][:, :], [(hT[:, hp, c, t * P:(t + 1) * P], wd_s[:, wp, c, :])
                                            for c in range(CHUNKS) for hp, wp in inner_terms], downed)

            def out(b, t):
                pe.wait_ge(aT_lo, START + (b + 1) * GROUPS)
                if t >= 2:
                    pe.wait_ge(y_done, START + b * TILES + t - 1)
                else:
                    pe.wait_ge((inv_back, attended)[t], START + (b + 1) * GROUPS)
                product((ps_t[0], ps_o)[t % 2][:, :], [(aT[:, ap, g, t * P:(t + 1) * P], wo_s[:, wp, g, :])
                                                    for g in range(GROUPS) for ap, wp in TERMS], outed)

            def steps(b, todo, inner_terms=TERMS, first=False):
                nb = 0 if first else b + 1
                for s in todo:
                    if s[0] == "score":
                        score(b, s[1])
                    elif s[0] == "turn_p":
                        turn_p(b, s[1])
                    elif s[0] == "values":
                        values(b, s[1])
                    elif s[0] == "turn_inv":
                        turn_inv(b, s[1])
                    elif s[0] == "gate":
                        inner_part(b, s[1], s[2], wg_s, ps_f[0], inner_g, gated, inner_terms)
                    elif s[0] == "up":
                        inner_part(b, s[1], s[2], wu_s, ps_f[1], inner_gu, upped, inner_terms)
                    elif s[0] == "down":
                        down(b, s[1], inner_terms)
                    elif s[0] == "out":
                        out(b, s[1])
                    elif s[0] == "turn_x":
                        turn_x(nb, s[1], first)
                    elif s[0] == "project":
                        project(nb if s[1] == 0 else b, s[1], s[2], s[3], first)
                    elif s[0] == "turn_qk":
                        turn_qk(nb if s[1] == 0 else b, s[1], s[2])

            for own in (scored, p_turned, valued, inv_turned, projected, qk_turned, gated, upped, x_turned,
                        downed, outed):
                pe.sem_inc(own, START)
            pe.wait_ge(consts_done, 6)
            pe.wait_ge(w_lo, len(pieces))
            steps(0, head_steps(), first=True)

            def batches(inner_terms):
                with pe.Fori(0, BATCH - 1) as b:
                    steps(b, main_steps(), inner_terms)
                    steps(b, tail_steps(True), inner_terms)
                steps(BATCH - 1, main_steps(), inner_terms)
                steps(BATCH - 1, tail_steps(False), inner_terms)

            pe.wait_ge(lo_known, 1)
            with pe.If(pe.value_load(lo_any[0:1, 0:1], min_val=0, max_val=1) > 0):
                batches(TERMS)
            with pe.Else():
                batches(TERMS[:2])

        @block.vector
        def _(dve):
            def ln(b, t):
                at = b * TILES + t
                dve.wait_ge(x_loaded[t % 2], (b * (TILES // 2) + t // 2 + 1) * 16)
                nc.vector.bn_stats(stats[:, t % 2, :], x_in[:, t % 2, :]).then_inc(stats_done, 1)
                dve.wait_ge(stats_done, START + at + 1)
                dve.sem_inc(dve_passed, 1)
                nc.vector.bn_aggr(mean_var[:, t % 2, :], stats[:, t % 2, :]).then_inc(var_done, 1)
                dve.wait_ge(rstd_done, START + 2 * at + 2)
                nc.vector.tensor_scalar(x_in[:, t % 2, :], x_in[:, t % 2, :], mean_var[:, t % 2, 0:1],
                                        rstd[:, t % 2, 1:2], ALU.subtract, ALU.mult).then_inc(x_normed, 1)

            def turn_x(b, t):
                dve.wait_ge(xT_hi, START + b * TILES + t + 1)
                nc.vector.tensor_tensor(xT[:, LO, :, t * P:(t + 1) * P],
                                        ps_s[t % 2][:, :].rearrange("p (k q) -> p k q", k=KT),
                                        xT[:, HI, :, t * P:(t + 1) * P], ALU.subtract).then_inc(xT_lo, 1)

            def project(b, g, t):
                a = b * ROWS + g * TILES + t
                dve.wait_ge(projected, START + a + 1)
                dve.wait_ge(qk_summed, START + a)
                src = ps_a[:, 0:2 * P].rearrange("p (n d) -> p n d", d=HD)
                cos, sin = (rope_s[:, t, k, :][:, None, :].broadcast_to([P, 2 * GH, HD]) for k in range(2))
                nc.vector.tensor_tensor(x_cos[:, :].rearrange("p (n d) -> p n d", d=HD), src, cos,
                                        ALU.mult).then_inc(rotated, 1)
                swapped = ps_a[:, 0:2 * P].rearrange("p (n d two) -> p n d two", two=2, d=HD // 2)[:, :, :, ::-1]
                sin = rope_s[:, t, 1, :].rearrange("p (d two) -> p d two", two=2)[:, None, :, :].broadcast_to(
                    [P, 2 * GH, HD // 2, 2])
                nc.vector.tensor_tensor(x_sin[:, :].rearrange("p (n d two) -> p n d two", two=2, d=HD // 2), swapped,
                                        sin, ALU.mult).then_inc(rotated, 1)

            def take_v(b, g, t):
                a = b * ROWS + g * TILES + t
                dve.wait_ge(v_hi, START + a + 1)
                nc.vector.scalar_tensor_tensor(v[:, g % 2, LO, t, :], ps_a[:, 2 * P:3 * P], QKV_OUT,
                                               v[:, g % 2, HI, t, :], ALU.mult, ALU.subtract).then_inc(v_lo, 1)

            def take_qk(b, g, t):
                a = b * ROWS + g * TILES + t
                dve.wait_ge(qk_turned, START + a + 1)
                dve.wait_ge(scored, START + b * UNITS + (g - 1) * TILES * GH if g else b * UNITS)
                bank = (turn_qk_at((g - 1) * TILES + t) + 1) % 2 if g else 1
                nc.vector.tensor_copy(qkT[:, g % 2, t, :, :, :].rearrange("p q h n -> p (q h n)"),
                                      ps_t[bank][:, :].bitcast(F16)).then_inc(qkT_done, 1)

            def score(b, n):
                g, i, h = unit(n)
                width = (i + 1) * P
                dve.wait_ge(scored, START + b * UNITS + n + 1)
                dve.sem_inc(dve_passed, 1)
                nc.vector.tensor_tensor_reduce(
                    out=ps_s[n % 2][:, 0:width], in0=ps_s[n % 2][:, 0:width], in1=mask[:, SEQ - width:SEQ],
                    scale=-SCORE, scalar=3.0e38, op0=ALU.add, op1=ALU.min,
                    accum_out=neg_max[:, n % 4:n % 4 + 1]).then_inc(max_done, 1)

            def take_p(b, n):
                g, i, h = unit(n)
                row, width = n // GH, (i + 1) * P
                dve.wait_ge(pT_hi, START + b * UNITS + n + 1)
                nc.vector.scalar_tensor_tensor(pT[:, row % 2, h, LO, 0:width], ps_t[n % 2][:, 0:width], P_SCALE,
                                               pT[:, row % 2, h, HI, 0:width], ALU.mult,
                                               ALU.subtract).then_inc(pT_lo, 1)

            def row_sums(b, g):
                dve.wait_ge(exp_done, START + b * UNITS + (g + 1) * TILES * GH)
                dve.wait_ge(inv_spread, START + b * GROUPS + g)
                nc.vector.reciprocal(inv[:, :], sums[:, g % 2, :]).then_inc(inv_done, 1)

            def norm(b, g):
                dve.wait_ge(inv_back, START + b * GROUPS + g + 1)
                dve.wait_ge(valued, START + b * ROWS + (g + 1) * TILES)
                nc.vector.tensor_tensor(spread[:, :], ps_o[:, :], spread[:, :], ALU.mult).then_inc(attended, 1)

            def times_gate(b, c):
                dve.wait_ge(tanh_done, START + b * CHUNKS + c + 1)
                dve.wait_ge(hT_lo, START + b * CHUNKS + (c - 1 if c >= 2 else 0))
                nc.vector.scalar_tensor_tensor(inner[:, c % 2, :], tanh[:, :], 1.0, ps_f[0][:, :], ALU.add,
                                               ALU.mult).then_inc(inner_g, 1)

            def times_up(b, c):
                dve.wait_ge(inner_g, START + b * CHUNKS + c + 1)
                dve.wait_ge(upped, START + b * CHUNKS + c + 1)
                nc.vector.scalar_tensor_tensor(inner[:, c % 2, :], inner[:, c % 2, :], gate_up[:, c:c + 1],
                                               ps_f[1][:, :], ALU.mult, ALU.mult).then_inc(inner_gu, 1)

            def down(b, t):
                dve.wait_ge(downed, START + b * TILES + t + 1)
                if t == 0:
                    dve.wait_ge(valued, START + (b + 1) * ROWS - 1)
                nc.vector.tensor_tensor(y[:, t, :], ps_f[t % 2][:, :], down_row[:, :], ALU.mult).then_inc(y_down, 1)

            def out(b, t):
                dve.wait_ge(outed, START + b * TILES + t + 1)
                dve.wait_ge(y_x, START + b * TILES + t + 1)
                nc.vector.scalar_tensor_tensor(y[:, t, :], (ps_t[0], ps_o)[t % 2][:, :], WO_OUT, y[:, t, :], ALU.mult,
                                               ALU.add).then_inc(y_done, 1)

            def steps(b, todo, first=False):
                nb = 0 if first else b + 1
                for s in todo:
                    if s[0] == "score":
                        score(b, s[1])
                    elif s[0] == "take_p":
                        take_p(b, s[1])
                    elif s[0] == "sums":
                        row_sums(b, s[1])
                    elif s[0] == "norm":
                        norm(b, s[1])
                    elif s[0] == "times_gate":
                        times_gate(b, s[1])
                    elif s[0] == "times_up":
                        times_up(b, s[1])
                    elif s[0] == "down":
                        down(b, s[1])
                    elif s[0] == "out":
                        out(b, s[1])
                    elif s[0] == "ln":
                        ln(nb, s[1])
                    elif s[0] == "turn_x":
                        turn_x(nb, s[1])
                    elif s[0] == "project" and s[3] == KT - 1:
                        project(nb if s[1] == 0 else b, s[1], s[2])
                    elif s[0] == "take_v":
                        take_v(nb if s[1] == 0 else b, s[1], s[2])
                    elif s[0] == "take_qk":
                        take_qk(nb if s[1] == 0 else b, s[1], s[2])

            for own in (stats_done, var_done, x_normed, xT_lo, rotated, v_lo, qkT_done, max_done, pT_lo,
                        inv_done, attended, inner_g, inner_gu, y_down, y_done):
                dve.sem_inc(own, START)
            dve.wait_ge(consts_loaded, 64)
            nc.vector.scalar_tensor_tensor(gate_up[:, :], gate_up[:, :], 0.5 * G_OUT * G_OUT * H_SCALE,
                                           gate_half[:, :], ALU.mult, ALU.mult).then_inc(scales_done, 1)
            nc.vector.tensor_scalar(down_row[:, :], down_row[:, :], D_OUT, None, ALU.mult).then_inc(scales_done, 1)
            dve.wait_ge(scales_done, 1)
            nc.vector.tensor_scalar(gate_half[:, :], gate_half[:, :], 0.5 * G_OUT, None,
                                    ALU.mult).then_inc(scales_done, 1)
            for k, (src, dst, scale, at, width) in enumerate(pieces):
                dve.wait_ge(w_hi, k + 1)
                nc.vector.scalar_tensor_tensor(flat(dst, LO)[:, at:at + width], staging[:, k % 2, 0:width], scale,
                                               flat(dst, HI)[:, at:at + width], ALU.mult,
                                               ALU.subtract).then_inc(w_lo, 1)
                if k >= first_inner:
                    dve.wait_ge(w_lo, k + 1)
                    nc.vector.tensor_reduce(lo_max[:, k - first_inner:k - first_inner + 1],
                                            flat(dst, LO)[:, at:at + width], mybir.AxisListType.X, ALU.max,
                                            apply_absolute_value=True).then_inc(lo_maxed, 1)
            dve.wait_ge(lo_maxed, inner_pieces)
            nc.vector.tensor_reduce(lo_most[:, 0:1], lo_max[:, 0:inner_pieces], mybir.AxisListType.X,
                                    ALU.max).then_inc(lo_maxed, 1)
            dve.wait_ge(lo_gathered, 1)
            nc.vector.tensor_scalar(lo_any[:, :], lo_most[:, 1:2], 0.0, None, ALU.is_gt).then_inc(lo_known, 1)
            dve.wait_ge(scales_done, 3)
            steps(0, head_steps(), first=True)
            with dve.Fori(0, BATCH - 1) as b:
                steps(b, main_steps())
                steps(b, tail_steps(True))
            steps(BATCH - 1, main_steps())
            steps(BATCH - 1, tail_steps(False))

        @block.scalar
        def _(act):
            def turn_x(b, t):
                act.wait_ge(x_turned, START + b * TILES + t + 1)
                if t == 0:
                    act.wait_ge(upped, START + b * CHUNKS)
                    act.wait_ge(projected, START + b * ROWS)
                nc.scalar.activation(xT[:, HI, :, t * P:(t + 1) * P],
                                     ps_s[t % 2][:, :].rearrange("p (k q) -> p k q", k=KT),
                                     ACT.Copy).then_inc(xT_hi, 1)

            def project(b, g, t):
                a = b * ROWS + g * TILES + t
                act.wait_ge(rotated, START + 2 * a + 2)
                if t == 0:
                    act.wait_ge(valued, START + b * ROWS + (g - 1) * TILES if g else b * ROWS)
                nc.scalar.activation(v[:, g % 2, HI, t, :], ps_a[:, 2 * P:3 * P], ACT.Copy,
                                     scale=QKV_OUT).then_inc(v_hi, 1)

            def split_qk(b, g, t, first=False):
                a = b * ROWS + g * TILES + t
                act.wait_ge(qk_summed, START + a + 1)
                if not (first and t < 2):
                    act.wait_ge(qk_turned, START + a - 1)
                for q in range(2):
                    src = qk[:, t % 2, q * P:(q + 1) * P].rearrange("p (h d) -> p h d", h=GH)
                    parts = qk_parts[:, t % 2, q, :, :, :]
                    parts = parts[:, :, 0:2, :] if q == 0 else parts[:, :, 0:4:2, :]
                    nc.scalar.activation(parts, src[:, :, None, :].broadcast_to([P, GH, 2, HD]),
                                         ACT.Copy).then_inc(qk_hi, 1)

            def exp(b, n):
                g, i, h = unit(n)
                width = (i + 1) * P
                act.wait_ge(max_done, START + b * UNITS + n + 1)
                act.wait_ge(p_turned, START + b * UNITS + (n - 1 if n >= 2 else 0))
                if n % (TILES * GH) == 0:
                    act.wait_ge(inv_done, START + b * GROUPS + (g - 1 if g else 0))
                nc.scalar.activation(probs[:, n % 2, 0:width], ps_s[n % 2][:, 0:width], ACT.Exp,
                                     bias=neg_max[:, n % 4:n % 4 + 1], scale=-1.0,
                                     accum_out=sums[:, g % 2, i * GH + h:i * GH + h + 1]).then_inc(exp_done, 1)

            def take_p(b, n):
                g, i, h = unit(n)
                row, width = n // GH, (i + 1) * P
                act.wait_ge(p_turned, START + b * UNITS + n + 1)
                if h == 0:
                    act.wait_ge(valued, START + b * ROWS + (row - 1 if row else 0))
                if n == 0:
                    act.wait_ge(stored, START + 16 * TILES * b)
                nc.scalar.activation(pT[:, row % 2, h, HI, 0:width], ps_t[n % 2][:, 0:width], ACT.Copy,
                                     scale=P_SCALE).then_inc(pT_hi, 1)

            def norm(b, g):
                act.wait_ge(inv_turned, START + b * GROUPS + g + 1)
                nc.scalar.activation(spread[:, :], ps_t[inv_bank(g)][:, :], ACT.Copy).then_inc(inv_back, 1)

            def take_a(b, g):
                act.wait_ge(attended, START + b * GROUPS + g + 1)
                if g == 0:
                    act.wait_ge(outed, START + b * TILES)
                nc.scalar.activation(aT[:, HI, g, :], spread[:, :], ACT.Copy).then_inc(aT_hi, 1)

            def gate(b, c):
                act.wait_ge(gated, START + b * CHUNKS + c + 1)
                act.wait_ge(inner_g, START + b * CHUNKS + c)
                nc.scalar.activation(tanh[:, :], ps_f[0][:, :], ACT.Tanh,
                                     scale=gate_half[:, c:c + 1]).then_inc(tanh_done, 1)

            def split_h(b, c):
                act.wait_ge(inner_gu, START + b * CHUNKS + c + 1)
                if c == 0:
                    act.wait_ge(downed, START + b * TILES)
                nc.scalar.activation(hT[:, HI, c, :], inner[:, c % 2, :], ACT.Copy).then_inc(hT_hi, 1)

            def steps(b, todo, first=False):
                nb = 0 if first else b + 1
                for s in todo:
                    if s[0] == "exp":
                        exp(b, s[1])
                    elif s[0] == "take_p":
                        take_p(b, s[1])
                    elif s[0] == "norm":
                        norm(b, s[1])
                    elif s[0] == "take_a":
                        take_a(b, s[1])
                    elif s[0] == "gate" and s[2] == KT - 1:
                        gate(b, s[1])
                    elif s[0] == "split_h":
                        split_h(b, s[1])
                    elif s[0] == "turn_x":
                        turn_x(nb, s[1])
                    elif s[0] == "project" and s[3] == KT - 1:
                        project(nb if s[1] == 0 else b, s[1], s[2])
                    elif s[0] == "split_qk":
                        split_qk(nb if s[1] == 0 else b, s[1], s[2], first)

            for own in (xT_hi, v_hi, qk_hi, exp_done, pT_hi, inv_back, aT_hi, tanh_done, hT_hi):
                act.sem_inc(own, START)
            for k, (src, dst, scale, at, width) in enumerate(pieces):
                act.wait_ge(w_loaded[k % 2], 16 * (k // 2 + 1))
                nc.scalar.activation(flat(dst, HI)[:, at:at + width], staging[:, k % 2, 0:width], ACT.Copy,
                                     scale=scale).then_inc(w_hi, 1)
            act.wait_ge(scales_done, 3)
            act.wait_ge(w_lo, len(pieces))
            steps(0, head_steps(), first=True)
            with act.Fori(0, BATCH - 1) as b:
                steps(b, main_steps())
                steps(b, tail_steps(True))
            steps(BATCH - 1, main_steps())
            steps(BATCH - 1, tail_steps(False))

        @block.gpsimd
        def _(pool):
            def ln(b, t, first=False):
                at = b * TILES + t
                pool.wait_ge(var_done, START + at + 1)
                if not (first and t < 2):
                    pool.wait_ge(x_normed, START + at - 1)
                pool.sem_inc(pool_passed, 1)
                nc.gpsimd.tensor_scalar(rstd[:, t % 2, 0:1], mean_var[:, t % 2, 1:2], EPS, X_SCALE ** -2, ALU.add,
                                        ALU.mult).then_inc(rstd_done, 1)
                pool.wait_ge(rstd_done, START + 2 * at + 1)
                nc.gpsimd.tensor_tensor(rstd[:, t % 2, 1:2], rstd[:, t % 2, 0:1], neg_half[:, :],
                                        ALU.pow).then_inc(rstd_done, 1)

            def project(b, g, t, first=False):
                a = b * ROWS + g * TILES + t
                pool.wait_ge(rotated, START + 2 * a + 2)
                if not (first and t < 2):
                    pool.wait_ge(qk_lo, START + 2 * a - 2)
                nc.gpsimd.tensor_tensor(qk[:, t % 2, :], x_cos[:, :], x_sin[:, :], ALU.add).then_inc(qk_summed, 1)

            def split_qk(b, g, t):
                a = b * ROWS + g * TILES + t
                for q in range(2):
                    pool.wait_ge(qk_hi, START + 2 * a + q + 1)
                    src = qk[:, t % 2, q * P:(q + 1) * P].rearrange("p (h d) -> p h d", h=GH)
                    parts = qk_parts[:, t % 2, q, :, :, :]
                    hi, lo = (parts[:, :, 0:2, :], parts[:, :, 2:4, :]) if q == 0 else (parts[:, :, 0:4:2, :],
                                                                                      parts[:, :, 1:4:2, :])
                    nc.gpsimd.tensor_tensor(lo, src[:, :, None, :].broadcast_to([P, GH, 2, HD]), hi,
                                            ALU.subtract).then_inc(qk_lo, 1)

            def row_sums(b, g):
                pool.wait_ge(inv_done, START + b * GROUPS + g + 1)
                pool.wait_ge(aT_lo, START + b * GROUPS + g)
                pool.sem_inc(pool_passed, 1)
                nc.gpsimd.tensor_scalar(spread[:, :].rearrange("p (n d) -> p n d", d=HD),
                                        inv[:, :][:, :, None].broadcast_to([P, TILES * GH, HD]), A_OUT, 1.0,
                                        ALU.mult, ALU.mult).then_inc(inv_spread, 1)

            def take_a(b, g):
                pool.wait_ge(aT_hi, START + b * GROUPS + g + 1)
                nc.gpsimd.tensor_tensor(aT[:, LO, g, :], spread[:, :], aT[:, HI, g, :],
                                        ALU.subtract).then_inc(aT_lo, 1)

            def split_h(b, c):
                pool.wait_ge(hT_hi, START + b * CHUNKS + c + 1)
                nc.gpsimd.tensor_tensor(hT[:, LO, c, :], inner[:, c % 2, :], hT[:, HI, c, :],
                                        ALU.subtract).then_inc(hT_lo, 1)

            def down(b, t):
                pool.wait_ge(y_down, START + b * TILES + t + 1)
                pool.wait_ge(res_loaded[t % 2], (b * (TILES // 2) + t // 2 + 1) * 16)
                nc.gpsimd.tensor_tensor(y[:, t, :], y[:, t, :], x_res[:, t % 2, :], ALU.add).then_inc(y_x, 1)

            def steps(b, todo, first=False):
                nb = 0 if first else b + 1
                for s in todo:
                    if s[0] == "sums":
                        row_sums(b, s[1])
                    elif s[0] == "take_a":
                        take_a(b, s[1])
                    elif s[0] == "split_h":
                        split_h(b, s[1])
                    elif s[0] == "down":
                        down(b, s[1])
                    elif s[0] == "ln":
                        ln(nb, s[1], first)
                    elif s[0] == "project" and s[3] == KT - 1:
                        project(nb if s[1] == 0 else b, s[1], s[2], first)
                    elif s[0] == "split_qk":
                        split_qk(nb if s[1] == 0 else b, s[1], s[2])

            for own in (rstd_done, qk_summed, qk_lo, inv_spread, aT_lo, hT_lo, y_x):
                pool.sem_inc(own, START)
            nc.gpsimd.memset(ident[:, :], 0.0).then_inc(consts_done, 1)
            nc.gpsimd.memset(mask[:, :], 0.0).then_inc(consts_done, 1)
            nc.gpsimd.memset(neg_half[:, :], -0.5).then_inc(consts_done, 1)
            pool.wait_ge(consts_done, 3)
            nc.gpsimd.affine_select(out=ident[:, :], in_=ident[:, :], compare_op=ALU.not_equal, fill=1.0, base=0,
                                    pattern=[[-1, P]], channel_multiplier=1).then_inc(consts_done, 1)
            nc.gpsimd.affine_select(out=mask[:, SEQ - P:SEQ], in_=mask[:, SEQ - P:SEQ], compare_op=ALU.is_ge,
                                    fill=MASKED, base=0, pattern=[[-1, P]],
                                    channel_multiplier=1).then_inc(consts_done, 1)
            pool.wait_ge(consts_done, 4)
            nc.gpsimd.tensor_copy(ident16[:, :], ident[:, :]).then_inc(consts_done, 1)
            pool.wait_ge(lo_maxed, inner_pieces + 1)
            nc.gpsimd.partition_all_reduce(lo_most[:, 1:2], lo_most[:, 0:1], P,
                                           bass.bass_isa.ReduceOp.max).then_inc(lo_gathered, 1)
            steps(0, head_steps(), first=True)
            with pool.Fori(0, BATCH - 1) as b:
                steps(b, main_steps())
                steps(b, tail_steps(True))
            steps(BATCH - 1, main_steps())
            steps(BATCH - 1, tail_steps(False))


def rope_table():
    freqs = np.exp(np.float32(-np.log(10000.0)) * np.arange(0, HD, 2, dtype=np.float32) / np.float32(HD))
    angles = np.arange(SEQ, dtype=np.float32)[:, None] * freqs.astype(np.float32)[None, :]
    cos = np.repeat(np.cos(angles), 2, axis=-1)
    sin = np.repeat(np.sin(angles), 2, axis=-1) * np.tile(np.float32([-1, 1]), HD // 2)
    table = np.stack([cos, sin], axis=1).astype(np.float32) * np.float32(QKV_OUT)
    return np.ascontiguousarray(table.reshape(TILES, P, 2, HD).transpose(1, 0, 2, 3))


def kernel(L0_attn_x, L0_attn_Wqkv, L0_attn_WO, L0_ffn_gate_w, L0_ffn_up_w, L0_ffn_down_w, L0_ffn_gate_s,
           L0_ffn_up_s, L0_ffn_down_s):
    import concourse.bacc as bacc
    from concourse.bass_utils import run_bass_kernel_spmd

    def by_partition(w):
        rows, cols = w.shape
        return np.ascontiguousarray(w.reshape(rows // P, P, cols).transpose(1, 0, 2).reshape(P, -1))

    qkv = np.asarray(L0_attn_Wqkv).T.reshape(DIM, 3, GROUPS, P).transpose(0, 2, 1, 3).reshape(DIM, 3 * DIM)
    arrays = {
        "x": np.ascontiguousarray(L0_attn_x),
        "wqkv": by_partition(qkv),
        "wo": by_partition(np.asarray(L0_attn_WO).T),
        "wg": by_partition(np.asarray(L0_ffn_gate_w).T),
        "wu": by_partition(np.asarray(L0_ffn_up_w).T),
        "wd": by_partition(np.asarray(L0_ffn_down_w).T),
        "gate_s": np.ascontiguousarray(np.asarray(L0_ffn_gate_s).reshape(CHUNKS, P).T),
        "up_s": np.ascontiguousarray(np.asarray(L0_ffn_up_s).reshape(CHUNKS, P).T),
        "down_s": np.ascontiguousarray(np.asarray(L0_ffn_down_s).reshape(1, DIM)),
        "rope": rope_table(),
    }
    nc = bacc.Bacc("TRN2", target_bir_lowering=False, num_devices=1)
    args = [nc.dram_tensor(f"{k}_dram", a.shape, mybir.dt.from_np(a.dtype), kind="ExternalInput").ap()
            for k, a in arrays.items()]
    y = nc.dram_tensor("y_dram", (BATCH, SEQ, DIM), F32, kind="ExternalOutput").ap()
    layer(nc, *args, y)
    r = run_bass_kernel_spmd(nc, [{f"{k}_dram": a for k, a in arrays.items()}], core_ids=[0])
    return r.results[0]["y_dram"]
```

```python
from contextlib import ExitStack

import numpy as np

import concourse.bass as bass

from concourse import mybir

F32 = mybir.dt.float32
F16 = mybir.dt.float16
BF16 = mybir.dt.bfloat16
ALU = mybir.AluOpType
ACT = mybir.ActivationFunctionType

P = 128
BATCH, SEQ, DIM = 8, 512, 512
HEADS, HD = 16, 32
INNER = 1408
TILES = SEQ // P
KT = DIM // P
GROUPS = HEADS * HD // P
GH = P // HD
CHUNKS = INNER // P
ROWS = GROUPS * TILES
UNITS = ROWS * GH
EPS = 1e-5
HI, LO = 0, 1
TERMS = ((HI, HI), (LO, HI), (HI, LO))

X_SCALE = 2.0 ** 8
W_SCALE = 2.0 ** 10
F_SCALE = 2.0 ** 6
QKV_SCALE = 2.0 ** 6
P_SCALE = 2.0 ** 10
A_SCALE = 2.0 ** 8
H_SCALE = 2.0 ** 4
QKV_OUT = QKV_SCALE / (X_SCALE * W_SCALE)
SCORE = HD ** -0.5 / QKV_SCALE ** 2
A_OUT = A_SCALE / (P_SCALE * QKV_SCALE)
WO_OUT = 1.0 / (A_SCALE * W_SCALE)
G_OUT = 1.0 / (X_SCALE * F_SCALE)
D_OUT = 1.0 / (H_SCALE * F_SCALE)
MASKED = -1e30
PROJECT_COST, TURN_COST, INNER_COST = 0.48, 0.5, 0.43
PIECES = (("wqkv", 6), ("wo", 2), ("wg", 8), ("wu", 8), ("wd", 8))
INNER_FIRST, PIECES_END = PIECES[0][1] + PIECES[1][1], sum(cut for _, cut in PIECES)
SLOTS = 4
INNER_PIECES = tuple(range(INNER_FIRST, PIECES_END))
HEAD_PIECES = ((6, 7), (8, 9), (10, 11))
LATE_PIECES = tuple(range(12, PIECES_END))
WEIGHTS_KNOWN_AT = len(LATE_PIECES) + 2
START = 1


def main_steps(more=True, first=False):
    a_tiles = [(1 + r // TILES, r % TILES) for r in range((GROUPS - 1) * TILES)]
    inner = [(kind, c, part) for c in range(CHUNKS) for kind in ("gate", "up") for part in range(KT)]
    inner_all = list(inner)
    share = (len(a_tiles) * (KT * PROJECT_COST + TURN_COST) + len(inner) * INNER_COST) / (UNITS - 1)
    inner_share = len(inner) * INNER_COST / (UNITS - WEIGHTS_KNOWN_AT - 1)
    out, later, sooner, spent = [("score", 0), ("exp", 0)], {}, {}, 0.0
    if more:
        later |= {UNITS - 14: [("ln", 0)], UNITS - 12: [("ln_x", 0)], UNITS - 10: [("ln", 1)], UNITS - 8: [("ln_x", 1)]}
    for n in range(UNITS):
        row, at = divmod(n, GH)
        if n + 1 < UNITS:
            out.append(("score", n + 1))
        out += sooner.pop(n, [])
        turned = [a_tiles[r] for r in range(len(a_tiles)) if n == turn_qk_at(r)]
        out += [("turn_qk", *x) for x in turned]
        spent += TURN_COST * len(turned)
        out += [("take_qk", *x) for x in turned]
        if n:
            out.append(("take_p", n - 1))
        if n + 1 < UNITS:
            out.append(("exp", n + 1))
        parts = ((0, 1), (2, 3), (), ())[at] if row < len(a_tiles) else ()
        spent += PROJECT_COST * len(parts)
        if first:
            spent = (len(inner_all) - len(inner)) * INNER_COST
            due = inner_share * (n - WEIGHTS_KNOWN_AT)
        else:
            due = share * (n + 1)
        while inner and (spent + INNER_COST / 2 < due or n == UNITS - 2):
            s = inner.pop(0)
            out.append(s)
            spent += INNER_COST
            if s[2] == KT - 1:
                soon = n if row >= len(a_tiles) else n + 1
                later.setdefault(soon, []).append((f"times_{s[0]}", s[1]))
                if s[0] == "up":
                    later.setdefault(soon + 1, []).append(("split_h", s[1]))
        if parts:
            out += [("project", *a_tiles[row], part) for part in parts]
            if parts == (2, 3):
                later.setdefault(n, []).append(("take_v", *a_tiles[row]))
                later.setdefault(n + 1, []).append(("split_qk", *a_tiles[row]))
        out.append(("turn_p", n))
        if first and n < len(LATE_PIECES):
            k = LATE_PIECES[n]
            out.append(("weights", k))
            later.setdefault(n + 1, []).append(("weights_max", k))
            early = k - len(LATE_PIECES)
            if early in INNER_PIECES and early not in LATE_PIECES:
                out.append(("weights_max", early))
        if first and n == WEIGHTS_KNOWN_AT:
            out.append(("weights_known",))
        out += later.pop(n, [])
        if n % (GH * TILES) == GH * TILES - 1:
            out.append(("sums", n // (GH * TILES)))
        if at == 1 and row:
            out.append(("values", row - 1))
            if row % TILES == 0:
                out.append(("turn_inv", row // TILES - 1))
                sooner.setdefault(n + 1, []).append(("norm", row // TILES - 1))
                later.setdefault(n + 2, []).insert(0, ("take_a", row // TILES - 1))
    for n in sorted(later):
        out += later[n]
    return out + [("take_p", UNITS - 1)]


def turn_qk_at(r):
    return GH * (r + 1) + 3


def tail_steps(more):
    a = [("turn_x", 0), ("turn_x", 1), ("ln", 2), ("ln_x", 2), ("ln", 3), ("ln_x", 3), ("down", 0),
         ("values", ROWS - 1), ("turn_inv", GROUPS - 1), ("norm", GROUPS - 1), ("turn_x", 2), ("turn_x", 3),
         ("take_a", GROUPS - 1), ("project", 0, 0), ("down", 1), ("project", 0, 1), ("split_qk", 0, 0), ("down", 2),
         ("turn_qk", 0, 0), ("take_qk", 0, 0), ("split_qk", 0, 1), ("down", 3), ("project", 0, 2), ("out", 0),
         ("turn_qk", 0, 1), ("take_qk", 0, 1), ("split_qk", 0, 2), ("out", 1), ("project", 0, 3),
         ("out", 2), ("turn_qk", 0, 2), ("take_qk", 0, 2), ("split_qk", 0, 3), ("out", 3), ("turn_qk", 0, 3),
         ("take_qk", 0, 3)]
    return whole(a if more else [s for s in a if s[0] in ("down", "out", "norm", "take_a", "turn_inv", "values")])


def head_steps():
    w = [("weights", k) for k in range(PIECES[0][1])]
    beside = [[("weights", k) for k in pieces] for pieces in HEAD_PIECES]
    return whole([
        ("ln", 0), w[0], ("ln", 1), w[1], ("ln_x", 0), ("turn_x", 0), w[2], ("ln_x", 1), ("turn_x", 1), w[3],
        ("ln", 2), w[4], ("ln", 3), w[5], ("project", 0, 0), ("ln_x", 2), ("turn_x", 2), ("split_qk", 0, 0),
        ("project", 0, 1), ("ln_x", 3), ("turn_x", 3), ("turn_qk", 0, 0), ("take_qk", 0, 0), ("split_qk", 0, 1),
        *beside[0], ("project", 0, 2), ("turn_qk", 0, 1), ("take_qk", 0, 1), ("split_qk", 0, 2), *beside[1],
        ("project", 0, 3), ("turn_qk", 0, 2), ("take_qk", 0, 2), ("split_qk", 0, 3), ("turn_qk", 0, 3),
        ("take_qk", 0, 3), *beside[2]])


def whole(steps):
    return [x for s in steps for x in ([(*s, part) for part in range(KT)] + [("take_v", *s[1:])]
                                       if s[0] == "project" else [s])]


def unit(n):
    return n // (TILES * GH), n // GH % TILES, n % GH


def layer(nc, x, wqkv, wo, wg, wu, wd, gate_s, up_s, down_s, rope, y_out):
    ctx = ExitStack()
    with ctx:
        def sb(name, shape, dtype):
            return ctx.enter_context(nc.sbuf_tensor(name, shape, dtype))

        def pb(name, shape, dtype):
            return ctx.enter_context(nc.psum_tensor(name, shape, dtype))

        def sem(name):
            return ctx.enter_context(nc.semaphore(name))

        wqkv_s = sb("wqkv_s", [P, 2, KT, GROUPS * 3 * P], F16)
        wo_s = sb("wo_s", [P, 2, GROUPS, DIM], F16)
        wg_s = sb("wg_s", [P, 2, KT, INNER], F16)
        wu_s = sb("wu_s", [P, 2, KT, INNER], F16)
        wd_s = sb("wd_s", [P, 2, CHUNKS, DIM], F16)
        ident = sb("ident", [P, P], F32)
        ident16 = sb("ident16", [P, P], F16)
        mask = sb("mask", [P, SEQ], BF16)
        rope_s = sb("rope_s", [P, TILES, 2, HD], F32)
        down_row = sb("down_row", [P, DIM], F32)
        gate_half = sb("gate_half", [P, CHUNKS], F32)
        gate_up = sb("gate_up", [P, CHUNKS], F32)
        neg_half = sb("neg_half", [P, 1], F32)
        lo_max = sb("lo_max", [P, len(INNER_PIECES) + 1], F32)
        lo_any = sb("lo_any", [P, 2], F32)
        lo_flag = sb("lo_flag", [P, 1], mybir.dt.int32)
        x_in = sb("x_in", [P, 2, DIM], F32)
        stats = sb("stats", [P, 2, 6], F32)
        mean_var = sb("mean_var", [P, 2, 2], F32)
        rstd = sb("rstd", [P, 2, 2], F32)
        xT = sb("xT", [P, 2, KT, SEQ], F16)
        x_cos = sb("x_cos", [P, 2 * P], F32)
        x_sin = sb("x_sin", [P, 2 * P], F32)
        qk = sb("qk", [P, 2, 2 * P], F32)
        qk_parts = sb("qk_parts", [P, 2, 2, GH, 4, HD], F16)
        qkT = sb("qkT", [P, 2, TILES, 2, GH, P], F16)
        v = sb("v", [P, 2, 2, TILES, P], F16)
        neg_max = sb("neg_max", [P, 4], F32)
        probs = sb("probs", [P, 2, SEQ], F32)
        pT = sb("pT", [P, 2, GH, 2, SEQ], F16)
        sums = sb("sums", [P, 2, TILES * GH], F32)
        inv = sb("inv", [P, TILES * GH], F32)
        spread = sb("spread", [P, SEQ], F32)
        aT = sb("aT", [P, 2, GROUPS, SEQ], F16)
        tanh = sb("tanh", [P, SEQ], F32)
        inner = sb("inner", [P, 2, SEQ], F32)
        hT = sb("hT", [P, 2, CHUNKS, SEQ], F16)
        x_res = sb("x_res", [P, 2, DIM], F32)
        y = pT[:, 0, :, :, :].rearrange("p h s q -> p (h s q)").bitcast(F32).rearrange("p (t d) -> p t d", t=TILES)
        staging = hT[:, :, :, :].rearrange("p s c q -> p (s c q)").bitcast(F32).rearrange("p (r w) -> p r w", r=SLOTS)

        ps_s = [pb("ps_s0", [P, 512], F32), pb("ps_s1", [P, 512], F32)]
        ps_t = [pb("ps_t0", [P, 512], F32), pb("ps_t1", [P, 512], F32)]
        ps_o = pb("ps_o", [P, 512], F32)
        ps_a = pb("ps_a", [P, 512], F32)
        ps_f = [pb("ps_f0", [P, 512], F32), pb("ps_f1", [P, 512], F32)]

        consts_loaded = sem("consts_loaded")
        consts_done = sem("consts_done")
        scales_done = sem("scales_done")
        w_loaded = [sem(f"w_loaded{k}") for k in range(SLOTS)]
        w_hi = sem("w_hi")
        w_lo = sem("w_lo")
        w_scaled = sem("w_scaled")
        inner_lo = sem("inner_lo")
        lo_maxed = sem("lo_maxed")
        lo_gathered = sem("lo_gathered")
        lo_known = sem("lo_known")
        x_loaded = [sem("x_loaded0"), sem("x_loaded1")]
        res_loaded = [sem("res_loaded0"), sem("res_loaded1")]
        stored = sem("stored")
        scored = sem("scored")
        p_turned = sem("p_turned")
        valued = sem("valued")
        inv_turned = sem("inv_turned")
        projected = sem("projected")
        qk_turned = sem("qk_turned")
        gated = sem("gated")
        upped = sem("upped")
        x_turned = sem("x_turned")
        downed = sem("downed")
        outed = sem("outed")
        stats_done = sem("stats_done")
        var_done = sem("var_done")
        x_normed = sem("x_normed")
        xT_lo = sem("xT_lo")
        rotated = sem("rotated")
        v_lo = sem("v_lo")
        qkT_done = sem("qkT_done")
        max_done = sem("max_done")
        pT_lo = sem("pT_lo")
        inv_done = sem("inv_done")
        attended = sem("attended")
        inner_g = sem("inner_g")
        inner_gu = sem("inner_gu")
        y_down = sem("y_down")
        y_done = sem("y_done")
        xT_hi = sem("xT_hi")
        v_hi = sem("v_hi")
        qk_hi = sem("qk_hi")
        exp_done = sem("exp_done")
        pT_hi = sem("pT_hi")
        inv_back = sem("inv_back")
        aT_hi = sem("aT_hi")
        tanh_done = sem("tanh_done")
        hT_hi = sem("hT_hi")
        rstd_done = sem("rstd_done")
        qk_summed = sem("qk_summed")
        qk_lo = sem("qk_lo")
        inv_spread = sem("inv_spread")
        aT_lo = sem("aT_lo")
        hT_lo = sem("hT_lo")
        y_x = sem("y_x")

        dve_passed = sem("dve_passed")
        pool_passed = sem("pool_passed")

        def flat(w, part):
            return w[:, part, :, :].rearrange("p a n -> p (a n)")

        named = {"wqkv": (wqkv, wqkv_s, W_SCALE), "wo": (wo, wo_s, W_SCALE), "wg": (wg, wg_s, F_SCALE),
                 "wu": (wu, wu_s, F_SCALE), "wd": (wd, wd_s, F_SCALE)}
        pieces = []
        for name, cut in PIECES:
            src, dst, scale = named[name]
            width = src.shape[1] // cut
            pieces += [(src, dst, scale, k * width, width) for k in range(cut)]
        first_pieces = PIECES[0][1]

        x_v = x.rearrange("b (t p) d -> b p t d", p=P)
        y_v = y_out.rearrange("b (t p) d -> b p t d", p=P)

        block = ctx.enter_context(nc.Block())

        @block.sync
        def _(sp):
            def load_x(b, t, wait=True):
                if wait:
                    sp.wait_ge(x_turned, START + b * TILES + t - 1)
                sp.dma_start(x_in[:, t % 2, :], x_v[b][:, t, :]).then_inc(x_loaded[t % 2], 16)

            def load_res(b, t):
                sp.wait_ge(y_x, START + b * TILES + (t - 1 if t >= 2 else 0))
                sp.dma_start(x_res[:, t % 2, :], x_v[b][:, t, :]).then_inc(res_loaded[t % 2], 16)

            def steps(b, todo):
                for s in todo:
                    if s == ("turn_x", 0) or s == ("turn_x", 1):
                        load_x(b + 1, s[1] + 2)
                    elif s == ("down", 0) or s == ("down", 1):
                        load_res(b, s[1] + 2)
                    elif s[0] == "out":
                        t = s[1]
                        sp.wait_ge(y_done, START + b * TILES + t + 1)
                        sp.dma_start(y_v[b][:, t, :], y[:, t, :]).then_inc(stored, 16)

            sp.sem_inc(stored, START)
            load_x(0, 0, wait=False)
            load_x(0, 1, wait=False)
            sp.dma_start(rope_s[:, :, :, :], rope).then_inc(consts_loaded, 16)
            sp.dma_start(gate_half[:, :], gate_s).then_inc(consts_loaded, 16)
            sp.dma_start(gate_up[:, :], up_s).then_inc(consts_loaded, 16)
            sp.dma_start(down_row[:, :], down_s.broadcast_to([P, DIM])).then_inc(consts_loaded, 16)
            for k, (src, dst, scale, at, width) in enumerate(pieces):
                if k == first_pieces:
                    load_x(0, 2)
                    load_x(0, 3)
                if k >= SLOTS:
                    if k - SLOTS < INNER_PIECES[0]:
                        sp.wait_ge(w_lo, k - SLOTS + 1)
                    else:
                        sp.wait_ge(inner_lo, k - SLOTS - INNER_PIECES[0] + 1)
                sp.dma_start(staging[:, k % SLOTS, 0:width], src[:, at:at + width]).then_inc(w_loaded[k % SLOTS], 16)

            def batch(b):
                load_res(b, 0)
                load_res(b, 1)
                load_x(b + 1, 0)
                load_x(b + 1, 1)
                steps(b, tail_steps(True))

            batch(0)
            with sp.Fori(1, BATCH - 1) as b:
                batch(b)
            load_res(BATCH - 1, 0)
            load_res(BATCH - 1, 1)
            steps(BATCH - 1, tail_steps(False))
            sp.wait_ge(stored, START + 16 * BATCH * TILES)

        @block.tensor
        def _(pe):
            def product(ps, pairs, sem_done):
                for k, (stationary, moving) in enumerate(pairs):
                    last = nc.tensor.matmul(ps, stationary, moving, start=(k == 0), stop=(k == len(pairs) - 1))
                last.then_inc(sem_done, 1)

            def turn_x(b, t, first=False):
                pe.wait_ge(x_normed, START + b * TILES + t + 1)
                if t >= 2:
                    pe.wait_ge(xT_lo, START + b * TILES + t - 1)
                elif not first:
                    pe.wait_ge(exp_done, START + (b - 1) * UNITS + UNITS - 1 + t)
                for k in range(KT):
                    last = nc.tensor.transpose(ps_s[t % 2][:, k * P:(k + 1) * P], x_in[:, t % 2, k * P:(k + 1) * P],
                                               ident[:, :])
                last.then_inc(x_turned, 1)

            def project(b, g, t, k, first=False):
                a = b * ROWS + g * TILES + t
                if k == 0:
                    pe.wait_ge(xT_lo, START + b * TILES + t + 1)
                    if not (first and t == 0):
                        pe.wait_ge(v_lo, START + a)
                        pe.wait_ge(qkT_done, START + (a if t == 0 and g < 2 else a - 1))
                for xp, wp in TERMS:
                    last = nc.tensor.matmul(ps_a[:, 0:3 * P], xT[:, xp, k, t * P:(t + 1) * P],
                                            wqkv_s[:, wp, k, g * 3 * P:(g + 1) * 3 * P],
                                            start=(k == 0 and (xp, wp) == TERMS[0]),
                                            stop=(k == KT - 1 and (xp, wp) == TERMS[-1]))
                if k == KT - 1:
                    last.then_inc(projected, 1)

            def turn_qk(b, g, t):
                a = b * ROWS + g * TILES + t
                pe.wait_ge(qk_lo, START + 2 * a + 2)
                pe.wait_ge(qkT_done, START + a)
                pe.wait_ge(v_lo, START + (a + 1 if t == TILES - 1 and g in (0, GROUPS - 1) else a + 2))
                into = ps_a[:, :].bitcast(F16)
                for q in range(2):
                    for h in range(GH):
                        last = nc.tensor.transpose(
                            into[:, (q * GH + h) * P:(q * GH + h + 1) * P],
                            qk_parts[:, t % 2, q, h, :, :].rearrange("p s d -> p (s d)"), ident16[:, :])
                last.then_inc(qk_turned, 1)

            def score(b, n):
                g, i, h = unit(n)
                pe.wait_ge(qkT_done, START + b * ROWS + n // GH + 1)
                if n < 2:
                    pe.wait_ge(xT_lo, START + b * TILES + TILES)
                else:
                    pe.wait_ge(exp_done, START + b * UNITS + n - 1)
                nc.tensor.matmul(ps_s[n % 2][:, 0:(i + 1) * P], qkT[:, g % 2, i, 0, h, :],
                                 qkT[:, g % 2, 0:i + 1, 1, h, :], start=True, stop=True).then_inc(scored, 1)

            def turn_p(b, n):
                g, i, h = unit(n)
                pe.wait_ge(exp_done, START + b * UNITS + n + 1)
                if n == 0:
                    pe.wait_ge(y_done, START + b * TILES)
                else:
                    pe.wait_ge(pT_lo, START + b * UNITS + max(n - 1, 0))
                if n > TILES * GH and n % (TILES * GH) == 2:
                    pe.wait_ge(inv_back, START + b * GROUPS + g)
                for j in range(i + 1):
                    last = nc.tensor.transpose(ps_t[n % 2][:, j * P:(j + 1) * P], probs[:, n % 2, j * P:(j + 1) * P],
                                               ident[:, :])
                last.then_inc(p_turned, 1)

            def values(b, row):
                g, i = divmod(row, TILES)
                pe.wait_ge(pT_lo, START + b * UNITS + (row + 1) * GH)
                pe.wait_ge(v_lo, START + b * ROWS + row + 1)
                if i == 0:
                    pe.wait_ge(attended, START + b * GROUPS + g)
                    pe.wait_ge(y_done, START + b * TILES)
                for j in range(i + 1):
                    for k, (pp, vp) in enumerate(TERMS):
                        for h in range(GH):
                            last = nc.tensor.matmul(
                                ps_o[h * HD:(h + 1) * HD, i * P:(i + 1) * P], v[:, g % 2, vp, j, h * HD:(h + 1) * HD],
                                pT[:, row % 2, h, pp, j * P:(j + 1) * P],
                                start=(j == 0 and k == 0), stop=(j == i and k == len(TERMS) - 1))
                last.then_inc(valued, 1)

            def turn_inv(b, g):
                pe.wait_ge(inv_spread, START + b * GROUPS + g + 1)
                n = min((g + 1) * TILES * GH + 1, UNITS - 1)
                pe.wait_ge(pT_lo, START + b * UNITS + n)
                for i in range(TILES):
                    last = nc.tensor.transpose(ps_t[0][:, i * P:(i + 1) * P], spread[:, i * P:(i + 1) * P],
                                               ident[:, :])
                last.then_inc(inv_turned, 1)

            def inner_part(b, c, k, w, ps, bank_read, sem_done, inner_terms):
                if k == 0:
                    pe.wait_ge(xT_lo, START + b * TILES + TILES)
                    pe.wait_ge(bank_read, START + b * CHUNKS + c)
                    if c == 0:
                        pe.wait_ge(y_down, START + b * TILES)
                for xp, wp in inner_terms:
                    last = nc.tensor.matmul(ps[:, :], w[:, wp, k, c * P:(c + 1) * P], xT[:, xp, k, :],
                                            start=(k == 0 and (xp, wp) == inner_terms[0]),
                                            stop=(k == KT - 1 and (xp, wp) == inner_terms[-1]))
                if k == KT - 1:
                    last.then_inc(sem_done, 1)

            def down(b, t, inner_terms):
                if t >= 2:
                    pe.wait_ge(y_down, START + b * TILES + t - 1)
                else:
                    pe.wait_ge((inner_g, inner_gu)[t], START + (b + 1) * CHUNKS)
                for c in range(CHUNKS):
                    if t == 0 and c >= CHUNKS - 2:
                        pe.wait_ge(hT_lo, START + b * CHUNKS + c + 1)
                    elif t == 0 and c == 0:
                        pe.wait_ge(hT_lo, START + (b + 1) * CHUNKS - 2)
                    for hp, wp in inner_terms:
                        last = nc.tensor.matmul(ps_f[t % 2][:, :], hT[:, hp, c, t * P:(t + 1) * P], wd_s[:, wp, c, :],
                                                start=(c == 0 and (hp, wp) == inner_terms[0]),
                                                stop=(c == CHUNKS - 1 and (hp, wp) == inner_terms[-1]))
                last.then_inc(downed, 1)

            def out(b, t):
                pe.wait_ge(aT_lo, START + (b + 1) * GROUPS)
                if t >= 2:
                    pe.wait_ge(y_done, START + b * TILES + t - 1)
                else:
                    pe.wait_ge((inv_back, attended)[t], START + (b + 1) * GROUPS)
                product((ps_t[0], ps_o)[t % 2][:, :], [(aT[:, ap, g, t * P:(t + 1) * P], wo_s[:, wp, g, :])
                                                    for g in range(GROUPS) for ap, wp in TERMS], outed)

            def steps(b, todo, inner_terms=TERMS, first=False):
                nb = 0 if first else b + 1
                for s in todo:
                    if s[0] == "score":
                        score(b, s[1])
                    elif s[0] == "turn_p":
                        turn_p(b, s[1])
                    elif s[0] == "values":
                        values(b, s[1])
                    elif s[0] == "turn_inv":
                        turn_inv(b, s[1])
                    elif s[0] == "gate":
                        inner_part(b, s[1], s[2], wg_s, ps_f[0], inner_g, gated, inner_terms)
                    elif s[0] == "up":
                        inner_part(b, s[1], s[2], wu_s, ps_f[1], inner_gu, upped, inner_terms)
                    elif s[0] == "down":
                        down(b, s[1], inner_terms)
                    elif s[0] == "out":
                        out(b, s[1])
                    elif s[0] == "turn_x":
                        turn_x(nb, s[1], first)
                    elif s[0] == "project":
                        project(nb if s[1] == 0 else b, s[1], s[2], s[3], first)
                    elif s[0] == "turn_qk":
                        turn_qk(nb if s[1] == 0 else b, s[1], s[2])

            for own in (scored, p_turned, valued, inv_turned, projected, qk_turned, gated, upped, x_turned,
                        downed, outed):
                pe.sem_inc(own, START)
            def batches(inner_terms):
                steps(0, first_main[known:], inner_terms)
                steps(0, tail_steps(True), inner_terms)
                with pe.Fori(1, BATCH - 1) as b:
                    steps(b, main_steps(), inner_terms)
                    steps(b, tail_steps(True), inner_terms)
                steps(BATCH - 1, main_steps(more=False), inner_terms)
                steps(BATCH - 1, tail_steps(False), inner_terms)

            pe.wait_ge(consts_done, 6)
            head = head_steps()
            start = head.index(("project", 0, 0, 0))
            steps(0, head[:start], first=True)
            pe.wait_ge(w_lo, first_pieces)
            steps(0, head[start:], first=True)
            first_main = main_steps(first=True)
            known = first_main.index(("weights_known",))
            steps(0, first_main[:known])
            pe.wait_ge(lo_known, 1)
            with pe.If(pe.value_load(lo_flag[0:1, 0:1], min_val=0, max_val=1) > 0):
                batches(TERMS)
            with pe.Else():
                batches(TERMS[:2])

        @block.vector
        def _(dve):
            def weights(k):
                src, dst, scale, at, width = pieces[k]
                lo = flat(dst, LO)[:, at:at + width]
                dve.wait_ge(w_hi, k + 1)
                nc.vector.scalar_tensor_tensor(lo, staging[:, k % SLOTS, 0:width], scale,
                                               flat(dst, HI)[:, at:at + width], ALU.mult,
                                               ALU.subtract).then_inc(w_lo, 1)

            def weights_max(k):
                src, dst, scale, at, width = pieces[k]
                n = INNER_PIECES.index(k)
                dve.wait_ge(inner_lo, n + 1)
                nc.vector.tensor_reduce(lo_max[:, n:n + 1], flat(dst, LO)[:, at:at + width], mybir.AxisListType.X,
                                        ALU.max, apply_absolute_value=True).then_inc(lo_maxed, 1)

            def weights_known():
                n = len(INNER_PIECES)
                dve.wait_ge(lo_maxed, n)
                nc.vector.tensor_reduce(lo_max[:, n:n + 1], lo_max[:, 0:n], mybir.AxisListType.X,
                                        ALU.max).then_inc(lo_maxed, 1)
                dve.wait_ge(lo_maxed, n + 1)
                nc.vector.tensor_scalar(lo_any[:, 0:1], lo_max[:, n:n + 1], 0.0, None,
                                        ALU.is_gt).then_inc(lo_maxed, 1)
                dve.wait_ge(lo_gathered, 1)
                nc.vector.tensor_copy(lo_flag[:, :], lo_any[:, 1:2]).then_inc(lo_known, 1)

            def ln(b, t):
                at = b * TILES + t
                dve.wait_ge(x_loaded[t % 2], (b * (TILES // 2) + t // 2 + 1) * 16)
                nc.vector.bn_stats(stats[:, t % 2, :], x_in[:, t % 2, :]).then_inc(stats_done, 1)
                dve.wait_ge(stats_done, START + at + 1)
                dve.sem_inc(dve_passed, 1)
                nc.vector.bn_aggr(mean_var[:, t % 2, :], stats[:, t % 2, :]).then_inc(var_done, 1)

            def ln_x(b, t):
                at = b * TILES + t
                dve.wait_ge(rstd_done, START + 2 * at + 2)
                nc.vector.tensor_scalar(x_in[:, t % 2, :], x_in[:, t % 2, :], mean_var[:, t % 2, 0:1],
                                        rstd[:, t % 2, 1:2], ALU.subtract, ALU.mult).then_inc(x_normed, 1)

            def turn_x(b, t):
                dve.wait_ge(xT_hi, START + b * TILES + t + 1)
                nc.vector.tensor_tensor(xT[:, LO, :, t * P:(t + 1) * P],
                                        ps_s[t % 2][:, :].rearrange("p (k q) -> p k q", k=KT),
                                        xT[:, HI, :, t * P:(t + 1) * P], ALU.subtract).then_inc(xT_lo, 1)

            def project(b, g, t):
                a = b * ROWS + g * TILES + t
                dve.wait_ge(projected, START + a + 1)
                dve.wait_ge(qk_summed, START + a)
                src = ps_a[:, 0:2 * P].rearrange("p (n d) -> p n d", d=HD)
                cos, sin = (rope_s[:, t, k, :][:, None, :].broadcast_to([P, 2 * GH, HD]) for k in range(2))
                nc.vector.tensor_tensor(x_cos[:, :].rearrange("p (n d) -> p n d", d=HD), src, cos,
                                        ALU.mult).then_inc(rotated, 1)
                swapped = ps_a[:, 0:2 * P].rearrange("p (n d two) -> p n d two", two=2, d=HD // 2)[:, :, :, ::-1]
                sin = rope_s[:, t, 1, :].rearrange("p (d two) -> p d two", two=2)[:, None, :, :].broadcast_to(
                    [P, 2 * GH, HD // 2, 2])
                nc.vector.tensor_tensor(x_sin[:, :].rearrange("p (n d two) -> p n d two", two=2, d=HD // 2), swapped,
                                        sin, ALU.mult).then_inc(rotated, 1)

            def take_v(b, g, t):
                a = b * ROWS + g * TILES + t
                dve.wait_ge(v_hi, START + a + 1)
                nc.vector.scalar_tensor_tensor(v[:, g % 2, LO, t, :], ps_a[:, 2 * P:3 * P], QKV_OUT,
                                               v[:, g % 2, HI, t, :], ALU.mult, ALU.subtract).then_inc(v_lo, 1)

            def take_qk(b, g, t):
                a = b * ROWS + g * TILES + t
                dve.wait_ge(qk_turned, START + a + 1)
                dve.wait_ge(scored, START + b * UNITS + (g - 1) * TILES * GH if g else b * UNITS)
                nc.vector.tensor_copy(qkT[:, g % 2, t, :, :, :].rearrange("p q h n -> p (q h n)"),
                                      ps_a[:, :].bitcast(F16)).then_inc(qkT_done, 1)

            def score(b, n):
                g, i, h = unit(n)
                width = (i + 1) * P
                dve.wait_ge(scored, START + b * UNITS + n + 1)
                dve.sem_inc(dve_passed, 1)
                nc.vector.tensor_tensor_reduce(
                    out=ps_s[n % 2][:, 0:width], in0=ps_s[n % 2][:, 0:width], in1=mask[:, SEQ - width:SEQ],
                    scale=-SCORE, scalar=3.0e38, op0=ALU.add, op1=ALU.min,
                    accum_out=neg_max[:, n % 4:n % 4 + 1]).then_inc(max_done, 1)

            def take_p(b, n):
                g, i, h = unit(n)
                row, width = n // GH, (i + 1) * P
                dve.wait_ge(pT_hi, START + b * UNITS + n + 1)
                nc.vector.scalar_tensor_tensor(pT[:, row % 2, h, LO, 0:width], ps_t[n % 2][:, 0:width], P_SCALE,
                                               pT[:, row % 2, h, HI, 0:width], ALU.mult,
                                               ALU.subtract).then_inc(pT_lo, 1)

            def row_sums(b, g):
                dve.wait_ge(exp_done, START + b * UNITS + (g + 1) * TILES * GH)
                dve.wait_ge(inv_spread, START + b * GROUPS + g)
                nc.vector.reciprocal(inv[:, :], sums[:, g % 2, :]).then_inc(inv_done, 1)

            def norm(b, g):
                dve.wait_ge(inv_back, START + b * GROUPS + g + 1)
                dve.wait_ge(valued, START + b * ROWS + (g + 1) * TILES)
                nc.vector.tensor_tensor(spread[:, :], ps_o[:, :], spread[:, :], ALU.mult).then_inc(attended, 1)

            def times_gate(b, c):
                dve.wait_ge(tanh_done, START + b * CHUNKS + c + 1)
                dve.wait_ge(hT_lo, START + b * CHUNKS + (c - 1 if c >= 2 else 0))
                nc.vector.scalar_tensor_tensor(inner[:, c % 2, :], tanh[:, :], 1.0, ps_f[0][:, :], ALU.add,
                                               ALU.mult).then_inc(inner_g, 1)

            def times_up(b, c):
                dve.wait_ge(inner_g, START + b * CHUNKS + c + 1)
                dve.wait_ge(upped, START + b * CHUNKS + c + 1)
                nc.vector.scalar_tensor_tensor(inner[:, c % 2, :], inner[:, c % 2, :], gate_up[:, c:c + 1],
                                               ps_f[1][:, :], ALU.mult, ALU.mult).then_inc(inner_gu, 1)

            def down(b, t):
                dve.wait_ge(downed, START + b * TILES + t + 1)
                if t == 0:
                    dve.wait_ge(valued, START + (b + 1) * ROWS - 1)
                nc.vector.tensor_tensor(y[:, t, :], ps_f[t % 2][:, :], down_row[:, :], ALU.mult).then_inc(y_down, 1)

            def out(b, t):
                dve.wait_ge(outed, START + b * TILES + t + 1)
                dve.wait_ge(y_x, START + b * TILES + t + 1)
                nc.vector.scalar_tensor_tensor(y[:, t, :], (ps_t[0], ps_o)[t % 2][:, :], WO_OUT, y[:, t, :], ALU.mult,
                                               ALU.add).then_inc(y_done, 1)

            def steps(b, todo, first=False):
                nb = 0 if first else b + 1
                for s in todo:
                    if s[0] == "score":
                        score(b, s[1])
                    elif s[0] == "weights" and s[1] not in INNER_PIECES:
                        weights(s[1])
                    elif s[0] == "weights_max":
                        weights_max(s[1])
                    elif s[0] == "weights_known":
                        weights_known()
                    elif s[0] == "take_p":
                        take_p(b, s[1])
                    elif s[0] == "sums":
                        row_sums(b, s[1])
                    elif s[0] == "norm":
                        norm(b, s[1])
                    elif s[0] == "times_gate":
                        times_gate(b, s[1])
                    elif s[0] == "times_up":
                        times_up(b, s[1])
                    elif s[0] == "down":
                        down(b, s[1])
                    elif s[0] == "out":
                        out(b, s[1])
                    elif s[0] == "ln":
                        ln(nb, s[1])
                    elif s[0] == "ln_x":
                        ln_x(nb, s[1])
                    elif s[0] == "turn_x":
                        turn_x(nb, s[1])
                    elif s[0] == "project" and s[3] == KT - 1:
                        project(nb if s[1] == 0 else b, s[1], s[2])
                    elif s[0] == "take_v":
                        take_v(nb if s[1] == 0 else b, s[1], s[2])
                    elif s[0] == "take_qk":
                        take_qk(nb if s[1] == 0 else b, s[1], s[2])

            for own in (stats_done, var_done, x_normed, xT_lo, rotated, v_lo, qkT_done, max_done, pT_lo,
                        inv_done, attended, inner_g, inner_gu, y_down, y_done):
                dve.sem_inc(own, START)
            dve.wait_ge(consts_loaded, 64)
            nc.vector.scalar_tensor_tensor(gate_up[:, :], gate_up[:, :], 0.5 * G_OUT * G_OUT * H_SCALE,
                                           gate_half[:, :], ALU.mult, ALU.mult).then_inc(scales_done, 1)
            nc.vector.tensor_scalar(down_row[:, :], down_row[:, :], D_OUT, None, ALU.mult).then_inc(scales_done, 1)
            dve.wait_ge(scales_done, 1)
            nc.vector.tensor_scalar(gate_half[:, :], gate_half[:, :], 0.5 * G_OUT, None,
                                    ALU.mult).then_inc(scales_done, 1)
            dve.wait_ge(scales_done, 3)
            steps(0, head_steps(), first=True)
            steps(0, main_steps(first=True))
            steps(0, tail_steps(True))
            with dve.Fori(1, BATCH - 1) as b:
                steps(b, main_steps())
                steps(b, tail_steps(True))
            steps(BATCH - 1, main_steps(more=False))
            steps(BATCH - 1, tail_steps(False))

        @block.scalar
        def _(act):
            def weights(k):
                src, dst, scale, at, width = pieces[k]
                act.wait_ge(w_loaded[k % SLOTS], 16 * (k // SLOTS + 1))
                if k in INNER_PIECES:
                    nc.scalar.activation(staging[:, k % SLOTS, 0:width], staging[:, k % SLOTS, 0:width], ACT.Copy,
                                         scale=scale).then_inc(w_scaled, 1)
                    act.wait_ge(w_scaled, INNER_PIECES.index(k) + 1)
                    scale = 1.0
                nc.scalar.activation(flat(dst, HI)[:, at:at + width], staging[:, k % SLOTS, 0:width], ACT.Copy,
                                     scale=scale).then_inc(w_hi, 1)

            def turn_x(b, t):
                act.wait_ge(x_turned, START + b * TILES + t + 1)
                if t == 0:
                    act.wait_ge(upped, START + b * CHUNKS)
                    act.wait_ge(projected, START + b * ROWS)
                nc.scalar.activation(xT[:, HI, :, t * P:(t + 1) * P],
                                     ps_s[t % 2][:, :].rearrange("p (k q) -> p k q", k=KT),
                                     ACT.Copy).then_inc(xT_hi, 1)

            def project(b, g, t):
                a = b * ROWS + g * TILES + t
                act.wait_ge(rotated, START + 2 * a + 2)
                if t == 0:
                    act.wait_ge(valued, START + b * ROWS + (g - 1) * TILES if g else b * ROWS)
                nc.scalar.activation(v[:, g % 2, HI, t, :], ps_a[:, 2 * P:3 * P], ACT.Copy,
                                     scale=QKV_OUT).then_inc(v_hi, 1)

            def split_qk(b, g, t, first=False):
                a = b * ROWS + g * TILES + t
                act.wait_ge(qk_summed, START + a + 1)
                if not (first and t < 2):
                    act.wait_ge(qk_turned, START + a - 1)
                for q in range(2):
                    src = qk[:, t % 2, q * P:(q + 1) * P].rearrange("p (h d) -> p h d", h=GH)
                    parts = qk_parts[:, t % 2, q, :, :, :]
                    parts = parts[:, :, 0:2, :] if q == 0 else parts[:, :, 0:4:2, :]
                    nc.scalar.activation(parts, src[:, :, None, :].broadcast_to([P, GH, 2, HD]),
                                         ACT.Copy).then_inc(qk_hi, 1)

            def exp(b, n):
                g, i, h = unit(n)
                width = (i + 1) * P
                act.wait_ge(max_done, START + b * UNITS + n + 1)
                act.wait_ge(p_turned, START + b * UNITS + (n - 1 if n >= 2 else 0))
                if n % (TILES * GH) == 0:
                    act.wait_ge(inv_done, START + b * GROUPS + (g - 1 if g else 0))
                nc.scalar.activation(probs[:, n % 2, 0:width], ps_s[n % 2][:, 0:width], ACT.Exp,
                                     bias=neg_max[:, n % 4:n % 4 + 1], scale=-1.0,
                                     accum_out=sums[:, g % 2, i * GH + h:i * GH + h + 1]).then_inc(exp_done, 1)

            def take_p(b, n):
                g, i, h = unit(n)
                row, width = n // GH, (i + 1) * P
                act.wait_ge(p_turned, START + b * UNITS + n + 1)
                if h == 0:
                    act.wait_ge(valued, START + b * ROWS + (row - 1 if row else 0))
                if n == 0:
                    act.wait_ge(stored, START + 16 * TILES * b)
                nc.scalar.activation(pT[:, row % 2, h, HI, 0:width], ps_t[n % 2][:, 0:width], ACT.Copy,
                                     scale=P_SCALE).then_inc(pT_hi, 1)

            def norm(b, g):
                act.wait_ge(inv_turned, START + b * GROUPS + g + 1)
                nc.scalar.activation(spread[:, :], ps_t[0][:, :], ACT.Copy).then_inc(inv_back, 1)

            def take_a(b, g):
                act.wait_ge(attended, START + b * GROUPS + g + 1)
                if g == 0:
                    act.wait_ge(outed, START + b * TILES)
                nc.scalar.activation(aT[:, HI, g, :], spread[:, :], ACT.Copy).then_inc(aT_hi, 1)

            def gate(b, c):
                act.wait_ge(gated, START + b * CHUNKS + c + 1)
                act.wait_ge(inner_g, START + b * CHUNKS + c)
                nc.scalar.activation(tanh[:, :], ps_f[0][:, :], ACT.Tanh,
                                     scale=gate_half[:, c:c + 1]).then_inc(tanh_done, 1)

            def split_h(b, c):
                act.wait_ge(inner_gu, START + b * CHUNKS + c + 1)
                if c == 0:
                    act.wait_ge(downed, START + b * TILES)
                nc.scalar.activation(hT[:, HI, c, :], inner[:, c % 2, :], ACT.Copy).then_inc(hT_hi, 1)

            def steps(b, todo, first=False):
                nb = 0 if first else b + 1
                for s in todo:
                    if s[0] == "weights":
                        weights(s[1])
                    elif s[0] == "weights_known":
                        act.wait_ge(inner_lo, len(INNER_PIECES))
                    elif s[0] == "exp":
                        exp(b, s[1])
                    elif s[0] == "take_p":
                        take_p(b, s[1])
                    elif s[0] == "norm":
                        norm(b, s[1])
                    elif s[0] == "take_a":
                        take_a(b, s[1])
                    elif s[0] == "gate" and s[2] == KT - 1:
                        gate(b, s[1])
                    elif s[0] == "split_h":
                        split_h(b, s[1])
                    elif s[0] == "turn_x":
                        turn_x(nb, s[1])
                    elif s[0] == "project" and s[3] == KT - 1:
                        project(nb if s[1] == 0 else b, s[1], s[2])
                    elif s[0] == "split_qk":
                        split_qk(nb if s[1] == 0 else b, s[1], s[2], first)

            for own in (xT_hi, v_hi, qk_hi, exp_done, pT_hi, inv_back, aT_hi, tanh_done, hT_hi):
                act.sem_inc(own, START)
            steps(0, head_steps(), first=True)
            act.wait_ge(scales_done, 3)
            steps(0, main_steps(first=True))
            steps(0, tail_steps(True))
            with act.Fori(1, BATCH - 1) as b:
                steps(b, main_steps())
                steps(b, tail_steps(True))
            steps(BATCH - 1, main_steps(more=False))
            steps(BATCH - 1, tail_steps(False))

        @block.gpsimd
        def _(pool):
            def weights(k):
                src, dst, scale, at, width = pieces[k]
                pool.wait_ge(w_hi, k + 1)
                nc.gpsimd.tensor_tensor(flat(dst, LO)[:, at:at + width], staging[:, k % SLOTS, 0:width],
                                        flat(dst, HI)[:, at:at + width], ALU.subtract).then_inc(inner_lo, 1)

            def ln(b, t, first=False):
                at = b * TILES + t
                pool.wait_ge(var_done, START + at + 1)
                if not (first and t < 2):
                    pool.wait_ge(x_normed, START + at - 1)
                pool.sem_inc(pool_passed, 1)
                nc.gpsimd.tensor_scalar(rstd[:, t % 2, 0:1], mean_var[:, t % 2, 1:2], EPS, X_SCALE ** -2, ALU.add,
                                        ALU.mult).then_inc(rstd_done, 1)
                pool.wait_ge(rstd_done, START + 2 * at + 1)
                nc.gpsimd.tensor_tensor(rstd[:, t % 2, 1:2], rstd[:, t % 2, 0:1], neg_half[:, :],
                                        ALU.pow).then_inc(rstd_done, 1)

            def project(b, g, t, first=False):
                a = b * ROWS + g * TILES + t
                pool.wait_ge(rotated, START + 2 * a + 2)
                if not (first and t < 2):
                    pool.wait_ge(qk_lo, START + 2 * a - 2)
                nc.gpsimd.tensor_tensor(qk[:, t % 2, :], x_cos[:, :], x_sin[:, :], ALU.add).then_inc(qk_summed, 1)

            def split_qk(b, g, t):
                a = b * ROWS + g * TILES + t
                for q in range(2):
                    pool.wait_ge(qk_hi, START + 2 * a + q + 1)
                    src = qk[:, t % 2, q * P:(q + 1) * P].rearrange("p (h d) -> p h d", h=GH)
                    parts = qk_parts[:, t % 2, q, :, :, :]
                    hi, lo = (parts[:, :, 0:2, :], parts[:, :, 2:4, :]) if q == 0 else (parts[:, :, 0:4:2, :],
                                                                                      parts[:, :, 1:4:2, :])
                    nc.gpsimd.tensor_tensor(lo, src[:, :, None, :].broadcast_to([P, GH, 2, HD]), hi,
                                            ALU.subtract).then_inc(qk_lo, 1)

            def row_sums(b, g):
                pool.wait_ge(inv_done, START + b * GROUPS + g + 1)
                pool.wait_ge(aT_lo, START + b * GROUPS + g)
                pool.sem_inc(pool_passed, 1)
                nc.gpsimd.tensor_scalar(spread[:, :].rearrange("p (n d) -> p n d", d=HD),
                                        inv[:, :][:, :, None].broadcast_to([P, TILES * GH, HD]), A_OUT, 1.0,
                                        ALU.mult, ALU.mult).then_inc(inv_spread, 1)

            def take_a(b, g):
                pool.wait_ge(aT_hi, START + b * GROUPS + g + 1)
                nc.gpsimd.tensor_tensor(aT[:, LO, g, :], spread[:, :], aT[:, HI, g, :],
                                        ALU.subtract).then_inc(aT_lo, 1)

            def split_h(b, c):
                pool.wait_ge(hT_hi, START + b * CHUNKS + c + 1)
                nc.gpsimd.tensor_tensor(hT[:, LO, c, :], inner[:, c % 2, :], hT[:, HI, c, :],
                                        ALU.subtract).then_inc(hT_lo, 1)

            def down(b, t):
                pool.wait_ge(y_down, START + b * TILES + t + 1)
                pool.wait_ge(res_loaded[t % 2], (b * (TILES // 2) + t // 2 + 1) * 16)
                nc.gpsimd.tensor_tensor(y[:, t, :], y[:, t, :], x_res[:, t % 2, :], ALU.add).then_inc(y_x, 1)

            def steps(b, todo, first=False):
                nb = 0 if first else b + 1
                for s in todo:
                    if s[0] == "weights" and s[1] in INNER_PIECES:
                        weights(s[1])
                    elif s[0] == "weights_known":
                        pool.wait_ge(lo_maxed, len(INNER_PIECES) + 2)
                        nc.gpsimd.partition_all_reduce(lo_any[:, 1:2], lo_any[:, 0:1], P,
                                                       bass.bass_isa.ReduceOp.max).then_inc(lo_gathered, 1)
                    elif s[0] == "sums":
                        row_sums(b, s[1])
                    elif s[0] == "take_a":
                        take_a(b, s[1])
                    elif s[0] == "split_h":
                        split_h(b, s[1])
                    elif s[0] == "down":
                        down(b, s[1])
                    elif s[0] == "ln":
                        ln(nb, s[1], first)
                    elif s[0] == "project" and s[3] == KT - 1:
                        project(nb if s[1] == 0 else b, s[1], s[2], first)
                    elif s[0] == "split_qk":
                        split_qk(nb if s[1] == 0 else b, s[1], s[2])

            for own in (rstd_done, qk_summed, qk_lo, inv_spread, aT_lo, hT_lo, y_x):
                pool.sem_inc(own, START)
            nc.gpsimd.memset(ident[:, :], 0.0).then_inc(consts_done, 1)
            nc.gpsimd.memset(mask[:, :], 0.0).then_inc(consts_done, 1)
            nc.gpsimd.memset(neg_half[:, :], -0.5).then_inc(consts_done, 1)
            pool.wait_ge(consts_done, 3)
            nc.gpsimd.affine_select(out=ident[:, :], in_=ident[:, :], compare_op=ALU.not_equal, fill=1.0, base=0,
                                    pattern=[[-1, P]], channel_multiplier=1).then_inc(consts_done, 1)
            nc.gpsimd.affine_select(out=mask[:, SEQ - P:SEQ], in_=mask[:, SEQ - P:SEQ], compare_op=ALU.is_ge,
                                    fill=MASKED, base=0, pattern=[[-1, P]],
                                    channel_multiplier=1).then_inc(consts_done, 1)
            pool.wait_ge(consts_done, 4)
            nc.gpsimd.tensor_copy(ident16[:, :], ident[:, :]).then_inc(consts_done, 1)
            steps(0, head_steps(), first=True)
            steps(0, main_steps(first=True))
            steps(0, tail_steps(True))
            with pool.Fori(1, BATCH - 1) as b:
                steps(b, main_steps())
                steps(b, tail_steps(True))
            steps(BATCH - 1, main_steps(more=False))
            steps(BATCH - 1, tail_steps(False))


def rope_table():
    freqs = np.exp(np.float32(-np.log(10000.0)) * np.arange(0, HD, 2, dtype=np.float32) / np.float32(HD))
    angles = np.arange(SEQ, dtype=np.float32)[:, None] * freqs.astype(np.float32)[None, :]
    cos = np.repeat(np.cos(angles), 2, axis=-1)
    sin = np.repeat(np.sin(angles), 2, axis=-1) * np.tile(np.float32([-1, 1]), HD // 2)
    table = np.stack([cos, sin], axis=1).astype(np.float32) * np.float32(QKV_OUT)
    return np.ascontiguousarray(table.reshape(TILES, P, 2, HD).transpose(1, 0, 2, 3))


def kernel(L0_attn_x, L0_attn_Wqkv, L0_attn_WO, L0_ffn_gate_w, L0_ffn_up_w, L0_ffn_down_w, L0_ffn_gate_s,
           L0_ffn_up_s, L0_ffn_down_s):
    import concourse.bacc as bacc
    from concourse.bass_utils import run_bass_kernel_spmd

    def by_partition(w):
        rows, cols = w.shape
        return np.ascontiguousarray(w.reshape(rows // P, P, cols).transpose(1, 0, 2).reshape(P, -1))

    qkv = np.asarray(L0_attn_Wqkv).T.reshape(DIM, 3, GROUPS, P).transpose(0, 2, 1, 3).reshape(DIM, 3 * DIM)
    arrays = {
        "x": np.ascontiguousarray(L0_attn_x),
        "wqkv": by_partition(qkv),
        "wo": by_partition(np.asarray(L0_attn_WO).T),
        "wg": by_partition(np.asarray(L0_ffn_gate_w).T),
        "wu": by_partition(np.asarray(L0_ffn_up_w).T),
        "wd": by_partition(np.asarray(L0_ffn_down_w).T),
        "gate_s": np.ascontiguousarray(np.asarray(L0_ffn_gate_s).reshape(CHUNKS, P).T),
        "up_s": np.ascontiguousarray(np.asarray(L0_ffn_up_s).reshape(CHUNKS, P).T),
        "down_s": np.ascontiguousarray(np.asarray(L0_ffn_down_s).reshape(1, DIM)),
        "rope": rope_table(),
    }
    nc = bacc.Bacc("TRN2", target_bir_lowering=False, num_devices=1)
    args = [nc.dram_tensor(f"{k}_dram", a.shape, mybir.dt.from_np(a.dtype), kind="ExternalInput").ap()
            for k, a in arrays.items()]
    y = nc.dram_tensor("y_dram", (BATCH, SEQ, DIM), F32, kind="ExternalOutput").ap()
    layer(nc, *args, y)
    r = run_bass_kernel_spmd(nc, [{f"{k}_dram": a for k, a in arrays.items()}], core_ids=[0])
    return r.results[0]["y_dram"]
```
